# Optimizing a Trainium2 kernel written in Bass

```python
import numpy as np
import jax
import jax.numpy as jnp

def _softmax(x, axis=-1):
    return jax.nn.softmax(x, axis=axis)

def _gelu(x):
    return jax.nn.gelu(x, approximate=True)

def _silu(x):
    return jax.nn.silu(x)

def _sigmoid(x):
    return jax.nn.sigmoid(x)

def _layernorm(x, axis=-1, eps=1e-05):
    m = jnp.mean(x, axis=axis, keepdims=True)
    v = jnp.var(x, axis=axis, keepdims=True)
    return (x - m) / jnp.sqrt(v + eps)

def _scatter_add(tgt, idx, src, axis=0):
    return tgt.at[idx].add(src)

def _segment_sum(src, seg, n):
    return jax.ops.segment_sum(src, seg, n)
kernel_name = 'mk_xattn_ffn_d1_seqx_r4_ef845e'

def setup_inputs(seed: int=0):
    np.random.seed(seed)
    _w = jnp.asarray

    def _rec_inputs():
        import jax
        import jax.numpy as jnp
        _rk = jax.random.key(seed)
        x = 7.22e-05 + 1 * jax.random.normal(jax.random.fold_in(_rk, 1), (64, 128, 256), jnp.float32)
        _lenS = 128 - jax.random.randint(jax.random.fold_in(_rk, 7), (64,), 0, max(1, 128 // 4) + 1, jnp.int32)
        _lenS2 = 128 - jax.random.randint(jax.random.fold_in(_rk, 8), (64,), 0, max(1, 128 // 4) + 1, jnp.int32)
        _ctx_1024P = jax.random.normal(jax.random.fold_in(_rk, 11), (64, 16, 256), jnp.float32)
        _ctx_1024c = jax.random.dirichlet(jax.random.fold_in(_rk, 511), 0.3 * jnp.ones((16,), jnp.float32), (64, 128))
        _ctx_1024t = jnp.einsum('bsk,bkd->bsd', _ctx_1024c, _ctx_1024P)
        _ctx_1024t = _ctx_1024t * jax.lax.rsqrt(jnp.mean(jnp.square(_ctx_1024t)) + 1e-12) * 0.953939
        ctx_1024 = 4.13588e-05 + 0.999923 * (_ctx_1024t + 0.3 * jax.random.normal(jax.random.fold_in(_rk, 611), (64, 128, 256), jnp.float32))
        return (x, ctx_1024)
    x, ctx_1024 = _rec_inputs()

    def _L0_xattn_setup():
        import jax, jax.numpy as jnp
        import numpy as np
        import math
        B, C, L = (16, 128, 256)
        key = jax.random.key(seed)
        kq, kk, kv = jax.random.split(key, 3)
        q = jax.random.normal(kq, (B, C, L), dtype=jnp.float32)
        k = jax.random.normal(kk, (B, C, L), dtype=jnp.float32)
        v = jax.random.normal(kv, (B, C, L), dtype=jnp.float32)
        return {'q': q, 'k': k, 'v': v}
    _L0_xattn_all = _L0_xattn_setup()
    _L0_xattn_in = {k: v for k, v in _L0_xattn_all.items() if k in ()}
    del _L0_xattn_all

    def _L0_ffn_setup():
        import jax, jax.numpy as jnp
        import numpy as np
        S, B, H, F, E, K = (512, 2, 256, 512, 8, 2)

        def _moe_forward(hidden_states, router_w, w1, b1, w2, b2):
            s, b, h = hidden_states.shape
            T = s * b
            x = hidden_states.reshape(T, h)
            logits = jnp.einsum('th,eh->te', x, router_w)
            topk_logits, topk_idx = jax.lax.top_k(logits, K)
            probs = jax.nn.softmax(topk_logits, axis=-1)
            combine = jnp.zeros((T, E), dtype=x.dtype)
            combine = combine.at[jnp.arange(T)[:, None], topk_idx].add(probs.astype(x.dtype))
            hmid = jnp.einsum('th,efh->etf', x, w1) + b1[:, None, :]
            hmid = jax.nn.gelu(hmid, approximate=False)
            y = jnp.einsum('etf,ehf->eth', hmid, w2) + b2[:, None, :]
            out = jnp.einsum('eth,te->th', y, combine)
            return out.reshape(s, b, h)
        key = jax.random.key(seed)
        ks = jax.random.split(key, 6)
        std = 0.02
        return {'hidden_states': jax.random.normal(ks[0], (S, B, H), dtype=jnp.float32), 'router_w': jax.random.normal(ks[1], (E, H), dtype=jnp.float32) * std, 'w1': jax.random.normal(ks[2], (E, F, H), dtype=jnp.float32) * (1.0 / np.sqrt(H)), 'b1': jnp.zeros((E, F), dtype=jnp.float32), 'w2': jax.random.normal(ks[3], (E, H, F), dtype=jnp.float32) * (1.0 / np.sqrt(F)), 'b2': jnp.zeros((E, H), dtype=jnp.float32)}
    _L0_ffn_all = _L0_ffn_setup()
    _L0_ffn_in = {k: v for k, v in _L0_ffn_all.items() if k in ('router_w', 'w1', 'b1', 'w2', 'b2')}
    del _L0_ffn_all
    return {'x': x, 'ctx_1024': ctx_1024, 'L0_ffn_router_w': _L0_ffn_in['router_w'], 'L0_ffn_w1': _L0_ffn_in['w1'], 'L0_ffn_b1': _L0_ffn_in['b1'], 'L0_ffn_w2': _L0_ffn_in['w2'], 'L0_ffn_b2': _L0_ffn_in['b2']}

def reference(x, ctx_1024, L0_ffn_router_w, L0_ffn_w1, L0_ffn_b1, L0_ffn_w2, L0_ffn_b2):
    import jax
    import jax.numpy as jnp

    def _L0_xattn_ref(q, k, v):
        import jax, jax.numpy as jnp
        import numpy as np
        import math
        B, C, L = (16, 128, 256)
        b, c, l = q.shape
        score = jnp.einsum('bci,bcj->bij', k, q) / math.sqrt(l)
        score = jax.nn.softmax(score, axis=0)
        out = jnp.einsum('bci,bij->bcj', v, score)
        return out

    def _L0_ffn_ref(hidden_states, router_w, w1, b1, w2, b2):
        import jax, jax.numpy as jnp
        import numpy as np
        S, B, H, F, E, K = (512, 2, 256, 512, 8, 2)

        def _moe_forward(hidden_states, router_w, w1, b1, w2, b2):
            s, b, h = hidden_states.shape
            T = s * b
            x = hidden_states.reshape(T, h)
            logits = jnp.einsum('th,eh->te', x, router_w)
            topk_logits, topk_idx = jax.lax.top_k(logits, K)
            probs = jax.nn.softmax(topk_logits, axis=-1)
            combine = jnp.zeros((T, E), dtype=x.dtype)
            combine = combine.at[jnp.arange(T)[:, None], topk_idx].add(probs.astype(x.dtype))
            hmid = jnp.einsum('th,efh->etf', x, w1) + b1[:, None, :]
            hmid = jax.nn.gelu(hmid, approximate=False)
            y = jnp.einsum('etf,ehf->eth', hmid, w2) + b2[:, None, :]
            out = jnp.einsum('eth,te->th', y, combine)
            return out.reshape(s, b, h)
        return _moe_forward(hidden_states, router_w, w1, b1, w2, b2)
    x = x + _L0_xattn_ref(_layernorm(x, axis=-1), ctx_1024, ctx_1024)
    x = x + _L0_ffn_ref(_layernorm(x, axis=-1), L0_ffn_router_w, L0_ffn_w1, L0_ffn_b1, L0_ffn_w2, L0_ffn_b2)
    return x

_drawn_inputs = setup_inputs


def setup_inputs(seed=0):
    import zlib

    import numpy as np

    out = dict(_drawn_inputs(seed))
    spreads = {'L0_ffn_b1': (0.0, 0.272), 'L0_ffn_b2': (0.0, 0.1)}
    factors = {}
    for name, (base, spread) in spreads.items():
        noise = np.random.default_rng([zlib.crc32(name.encode()), seed]).standard_normal(out[name].shape)
        drawn = base * np.exp(spread * noise) if base else spread * noise
        out[name] = jnp.asarray(drawn.astype(out[name].dtype))
    for name, factor in factors.items():
        out[name] = (out[name] * factor).astype(out[name].dtype)
    return out
```

```python
from contextlib import ExitStack

import concourse.bass as bass
from concourse import mybir

F32 = mybir.dt.float32
F16 = mybir.dt.float16
I32 = mybir.dt.int32
U32 = mybir.dt.uint32
ALU = mybir.AluOpType
ACT = mybir.ActivationFunctionType
AX_X = mybir.AxisListType.X

P = 128
BATCH, ROWS, DIM = 64, 128, 256
EXPERTS, HID = 8, 512
TOKENS = BATCH * ROWS
HC = DIM // P
FC = HID // P
GROUP = 256
SUB = GROUP // P
GROUPS = TOKENS // GROUP + EXPERTS - 1
TILES = GROUPS * SUB
ROUNDS = 2
WSCALE = 64.0
SCORE_SCALE = 1.0 / 16.0
LN_EPS = 1e-5
ROW = 2 * DIM + 2
X2 = DIM
PR = 2 * DIM
ON_POOL = 192
SKIPPED = 16384
RING = 4


def pipeline(eng, count, unroll, peel, last_lag, body):
    for k in range(peel):
        body(0, k, "head")
    whole = peel + (count - peel) // unroll * unroll
    if whole > peel:
        with eng.Fori(peel // unroll, whole // unroll) as block:
            i = eng.snap(block * unroll)
            for k in range(unroll):
                body(i, k, "loop")
    for k in range(count - whole + last_lag):
        body(whole, k, "tail")


def wait_apart(eng, sem, count):
    if not isinstance(count, int):
        eng.lower_val(count)
    eng.wait_ge(sem, 1)
    eng.wait_ge(sem, count)


def live(i, k, lag, count):
    return not isinstance(i, int) or 0 <= i + k - lag < count


def xattn_ffn(nc, x, ctx, router_w, w1, b1, w2, b2, out):
    x_rows = x.rearrange("b c l -> (b c) l")
    ctx_rows = ctx.rearrange("b c l -> (b c) l")
    w1_rows = w1.rearrange("e f h -> (e f) h")
    w2_rows = w2.rearrange("e h f -> (e h) f")
    out_rows = out.rearrange("b c l -> (b c) l")
    table = [nc.dram_tensor("rows_first", [TOKENS, ROW], F32, kind="Internal").ap(),
             nc.dram_tensor("rows_second", [TOKENS, ROW], F32, kind="Internal").ap()]

    with ExitStack() as stack:
        def sb(name, shape, dt=F32):
            return stack.enter_context(nc.sbuf_tensor(name, shape, dt))

        def sem(name):
            return stack.enter_context(nc.semaphore(name))

        def sems(name, n):
            return [sem(f"{name}{i}") for i in range(n)]

        slots = sb("slots", [P, BATCH * ROW])
        w1T = [[[sb(f"w1T_{h}_{f}_{p}", [P, EXPERTS * P], F16) for p in range(2)] for f in range(FC)] for h in range(HC)]
        w2T = [[sb(f"w2T_{f}_{p}", [P, EXPERTS * DIM], F16) for p in range(2)] for f in range(FC)]
        smax = sb("smax", [P, 2 * DIM])
        ssum = sb("ssum", [P, 2 * DIM])
        ring4k = sb("ring4k", [P, RING, DIM])
        xring = sb("xring", [P, RING, DIM])
        ctxT = sb("ctxT", [P, 2, DIM])
        xn = sb("xn", [P, 2, DIM])
        xnT = sb("xnT", [P, 2, DIM])
        ident = sb("ident", [P, P])
        ident16 = sb("ident16", [P, P], F16)
        before = sb("before", [P, P], F16)
        ones16 = sb("ones16", [P, P], F16)
        iota16 = sb("iota16", [P, P], F16)
        iota_b1 = sb("iota_b1", [P, BATCH])
        iota_e = sb("iota_e", [P, EXPERTS])
        iota_g = sb("iota_g", [1, GROUPS])
        row_no1 = sb("row_no1", [P, 1])
        neg_half = sb("neg_half", [P, 1])
        rwT = sb("rwT", [P, HC, EXPERTS])
        b1T = sb("b1T", [P, EXPERTS, FC])
        rw_in = sb("rw_in", [EXPERTS, DIM])
        stats = sb("stats", [P, RING, 6])
        mv = sb("mv", [P, RING, 2])
        veps = sb("veps", [P, RING])
        rstd = sb("rstd", [P, RING])
        shift = sb("shift", [P, RING])
        top = sb("top", [P, RING, 8])
        topi = sb("topi", [P, RING, 8], U32)
        gap = sb("gap", [P, RING])
        egap = sb("egap", [P, RING])
        den = sb("den", [P, RING])
        choice = sb("choice", [P, ROUNDS, BATCH])
        ps = [stack.enter_context(nc.psum_tensor(f"ps{i}", [P, 512], F32)) for i in range(8)]

        def slot(b, first, n):
            return slots[:, bass.ds(b * ROW + first, n)]

        s_const = sem("s_const")
        s_small = sems("s_small", 2)
        s_setT = sem("s_setT")
        s_setc = sem("s_setc")
        b1_in = slots[0:EXPERTS, (BATCH - 1) * ROW:(BATCH - 1) * ROW + HID]
        with nc.Block() as block:
            @block.sync
            def _(sp):
                sp.dma_start(rw_in[:], router_w).then_inc(s_small[0], 16)
                sp.dma_start(b1_in, b1).then_inc(s_small[1], 16)

            @block.gpsimd
            def _(pool):
                pool.memset(ident[:], 0.0).then_inc(s_const, 1)
                pool.memset(ident16[:], 0.0).then_inc(s_const, 1)
                pool.memset(before[:], 0.0).then_inc(s_const, 1)
                pool.memset(ones16[:], 1.0).then_inc(s_const, 1)
                pool.memset(neg_half[:], -0.5).then_inc(s_const, 1)
                pool.memset(ssum[:], 0.0).then_inc(s_const, 1)
                pool.wait_ge(s_const, 6)
                for m in (ident, ident16):
                    pool.affine_select(out=m[:], in_=m[:], pattern=[[-1, P]], compare_op=ALU.not_equal, fill=1.0,
                                       base=0, channel_multiplier=1).then_inc(s_const, 1)
                pool.affine_select(out=before[:], in_=before[:], pattern=[[-1, P]], compare_op=ALU.is_ge, fill=1.0,
                                   base=0, channel_multiplier=1).then_inc(s_const, 1)
                pool.iota(iota16[:], [[1, P]], base=0, channel_multiplier=0, allow_small_or_imprecise_dtypes=True).then_inc(s_const, 1)
                pool.iota(iota_b1[:], [[1, BATCH]], base=0, channel_multiplier=0, allow_small_or_imprecise_dtypes=True).then_inc(s_const, 1)
                pool.iota(iota_e[:], [[1, EXPERTS]], base=0, channel_multiplier=0, allow_small_or_imprecise_dtypes=True).then_inc(s_const, 1)
                pool.iota(iota_g[:], [[1, GROUPS]], base=0, channel_multiplier=0, allow_small_or_imprecise_dtypes=True).then_inc(s_const, 1)
                pool.iota(row_no1[:], [[0, 1]], base=1, channel_multiplier=1, allow_small_or_imprecise_dtypes=True).then_inc(s_const, 1)

            @block.tensor
            def _(pe):
                pe.wait_ge(s_const, 14)
                pe.wait_ge(s_small[0], 16)
                for h in range(HC):
                    pe.transpose(ps[0][:, h * 8:h * 8 + 8], rw_in[:, h * P:(h + 1) * P], ident[0:8, 0:8]).then_inc(s_setT, 1)
                pe.wait_ge(s_small[1], 16)
                for f in range(FC):
                    pe.transpose(ps[1][:, f * 8:f * 8 + 8], b1_in[:, f * P:(f + 1) * P], ident[0:8, 0:8]).then_inc(s_setT, 1)

            @block.vector
            def _(dve):
                dve.wait_ge(s_setT, HC + FC)
                dve.tensor_copy(rwT[:].rearrange("p h e -> p (h e)"), ps[0][:, 0:HC * 8]).then_inc(s_setc, 1)
                dve.tensor_copy(b1T[:].rearrange("p e f -> p f e"), ps[1][:, 0:FC * 8].rearrange("p (f e) -> p f e", e=8)).then_inc(s_setc, 1)

        U1, LAG1 = 8, 3
        m_x_in = sems("m_x_in", RING)
        m_ctx_in = sems("m_ctx_in", RING)
        m_w_in = sems("m_w_in", 2)
        m_stat = sem("m_stat")
        m_mean = sem("m_mean")
        m_norm = sem("m_norm")
        m_q = sem("m_q")
        m_score = sem("m_score")
        m_max = sem("m_max")
        m_wT = sem("m_wT")
        m_whigh = sem("m_whigh")
        m_wlow = sem("m_wlow")

        def normalise_on_pool(pool, ready, value, k, done, steps, step_base):
            wait_apart(pool, ready, value)
            pool.tensor_scalar(veps[:, k:k + 1], mv[:, k, 1:2], LN_EPS, None, ALU.add).then_inc(steps, 1)
            pool.wait_ge(steps, step_base + 1)
            pool.tensor_tensor(rstd[:, k:k + 1], veps[:, k:k + 1], neg_half[:], ALU.pow).then_inc(steps, 1)
            wait_apart(pool, steps, step_base + 2)
            pool.tensor_scalar(shift[:, k:k + 1], mv[:, k, 0:1], rstd[:, k:k + 1], -1.0, ALU.mult, ALU.mult).then_inc(done, 1)

        m_pstep = sem("m_pstep")
        with nc.Block() as block:
            @block.sync
            def _(sp):
                def body(i, k, phase):
                    b, r = i + k, k % RING
                    if not (phase == "head" and k < RING):
                        sp.wait_ge(m_score, b - RING + 1)
                    sp.dma_start(slot(b, 0, DIM), x_rows[bass.ds(b * ROWS, ROWS), :]).then_inc(m_x_in[r], 16)
                    sp.dma_start(xring[:, r, :], ctx_rows[bass.ds(b * ROWS, ROWS), :]).then_inc(m_ctx_in[r], 16)
                    if k % 4 == 0:
                        half = (k // 4) % 2
                        if not (phase == "head" and k == 0):
                            sp.wait_ge(m_wT, b * 2)
                        sp.dma_start(ring4k[:, 0:2, :], w1_rows[bass.ds(b * 64, 2 * P), :].rearrange("(q p) h -> p q h", p=P)).then_inc(m_w_in[0], 16)
                        sp.dma_start(ring4k[:, 2:4, :].rearrange("p a b -> p (a b)"), w2_rows[bass.ds(b * 32, P), :]).then_inc(m_w_in[1], 16)
                pipeline(sp, BATCH, U1, U1, 0, body)

            @block.vector
            def _(dve):
                def body(i, k, phase):
                    if live(i, k, 0, BATCH):
                        b, r = i + k, k % RING
                        wait_apart(dve, m_x_in[r], 4 * b + 16 - 4 * r)
                        dve.bn_stats(stats[:, r, :], slot(b, 0, DIM)).then_inc(m_stat, 1)
                        wait_apart(dve, m_stat, b + 1)
                        dve.bn_aggr(mv[:, r, :], stats[:, r, :]).then_inc(m_mean, 1)
                    if live(i, k, LAG1, BATCH):
                        b, r = i + k - LAG1, (k - LAG1) % RING
                        dve.wait_ge(m_score, b + 1)
                        if phase == "head" and k == LAG1:
                            dve.tensor_copy(smax[:], ps[r][:]).then_inc(m_max, 1)
                        else:
                            dve.wait_ge(m_max, b)
                            dve.tensor_tensor(smax[:], ps[r][:], smax[:], ALU.max).then_inc(m_max, 1)
                    if k % 4 == 2 and live(i, k, 2, BATCH):
                        e, half = (i + k) // 8 if isinstance(i, int) else i // 8, k // 4
                        dve.wait_ge(m_whigh, 2 * (i + k - 2) + 4)
                        for q in range(2):
                            for h in range(HC):
                                dve.scalar_tensor_tensor(
                                    w1T[h][2 * half + q][1][:, bass.ds(e * P, P)], ps[4][:, (q * HC + h) * P:(q * HC + h + 1) * P], WSCALE,
                                    w1T[h][2 * half + q][0][:, bass.ds(e * P, P)], ALU.mult, ALU.subtract).then_inc(m_wlow, 1)
                        dve.wait_ge(m_whigh, 2 * (i + k - 2) + 8)
                        for f in range(FC):
                            dve.scalar_tensor_tensor(
                                w2T[f][1][:, bass.ds(e * DIM + half * P, P)], ps[5][:, f * P:(f + 1) * P], WSCALE,
                                w2T[f][0][:, bass.ds(e * DIM + half * P, P)], ALU.mult, ALU.subtract).then_inc(m_wlow, 1)
                pipeline(dve, BATCH, U1, U1, LAG1, body)

            @block.gpsimd
            def _(pool):
                def body(i, k, phase):
                    b, r = i + k, k % RING
                    normalise_on_pool(pool, m_mean, b + 1, r, m_norm, m_pstep, 2 * b)
                pipeline(pool, BATCH, U1, U1, 0, body)

            @block.scalar
            def _(act):
                def body(i, k, phase):
                    b, r = i + k, k % RING
                    act.wait_ge(m_norm, b + 1)
                    act.activation(slot(b, 0, DIM), slot(b, 0, DIM), ACT.Identity, bias=shift[:, r:r + 1],
                                   scale=rstd[:, r:r + 1]).then_inc(m_q, 1)
                    if k % 4 == 1:
                        e, half = (i + k) // 8 if isinstance(i, int) else i // 8, k // 4
                        act.wait_ge(m_wT, 2 * (i + k - 1) + 4)
                        for q in range(2):
                            for h in range(HC):
                                act.activation(w1T[h][2 * half + q][0][:, bass.ds(e * P, P)],
                                               ps[4][:, (q * HC + h) * P:(q * HC + h + 1) * P], ACT.Copy, scale=WSCALE).then_inc(m_whigh, 1)
                        act.wait_ge(m_wT, 2 * (i + k - 1) + 8)
                        for f in range(FC):
                            act.activation(w2T[f][0][:, bass.ds(e * DIM + half * P, P)], ps[5][:, f * P:(f + 1) * P],
                                           ACT.Copy, scale=WSCALE).then_inc(m_whigh, 1)
                pipeline(act, BATCH, U1, U1, 0, body)

            @block.tensor
            def _(pe):
                def body(i, k, phase):
                    b, r = i + k, k % RING
                    if k % 4 == 0:
                        n = b // 4 if isinstance(i, int) else i // 4 + k // 4
                        pe.wait_ge(m_w_in[0], 16 * n + 16)
                        if not (phase == "head" and k == 0):
                            pe.wait_ge(m_wlow, 2 * b)
                        for q in range(2):
                            for h in range(HC):
                                pe.transpose(ps[4][:, (q * HC + h) * P:(q * HC + h + 1) * P], ring4k[:, q, h * P:(h + 1) * P], ident[:]).then_inc(m_wT, 1)
                        pe.wait_ge(m_w_in[1], 16 * n + 16)
                        for f in range(FC):
                            pe.transpose(ps[5][:, f * P:(f + 1) * P], ring4k[:, 2 + f // 2, (f % 2) * P:(f % 2 + 1) * P], ident[:]).then_inc(m_wT, 1)
                    pe.wait_ge(m_ctx_in[r], 4 * b + 16 - 4 * r)
                    pe.wait_ge(m_q, b + 1)
                    if not (phase == "head" and k < RING):
                        pe.wait_ge(m_max, b - RING + 1)
                    for h in range(HC):
                        mm = pe.matmul(ps[r][:, h * DIM:(h + 1) * DIM], xring[:, r, h * P:(h + 1) * P], slot(b, 0, DIM), start=True, stop=True)
                    mm.then_inc(m_score, 1)
                pipeline(pe, BATCH, U1, U1, 0, body)

        LAG2 = 2
        e_ctx_in = sems("e_ctx_in", RING)
        e_score = sem("e_score")
        e_diff = sem("e_diff")
        e_exp = sem("e_exp")
        e_sumv = sem("e_sumv")
        e_sump = sem("e_sump")
        with nc.Block() as block:
            @block.sync
            def _(sp):
                def body(i, k, phase):
                    b, r = i + k, k % RING
                    if not (phase == "head" and k < RING):
                        sp.wait_ge(e_score, b - RING + 1)
                    sp.dma_start(ring4k[:, r, :], ctx_rows[bass.ds(b * ROWS, ROWS), :]).then_inc(e_ctx_in[r], 16)
                pipeline(sp, BATCH, RING, RING, 0, body)

            @block.tensor
            def _(pe):
                def body(i, k, phase):
                    b, r = i + k, k % RING
                    pe.wait_ge(e_ctx_in[r], 4 * b + 16 - 4 * r)
                    if not (phase == "head" and k < RING):
                        pe.wait_ge(e_diff, b - RING + 1)
                    for h in range(HC):
                        mm = pe.matmul(ps[r][:, h * DIM:(h + 1) * DIM], ring4k[:, r, h * P:(h + 1) * P], slot(b, 0, DIM), start=True, stop=True)
                    mm.then_inc(e_score, 1)
                pipeline(pe, BATCH, RING, RING, 0, body)

            @block.vector
            def _(dve):
                def body(i, k, phase):
                    if live(i, k, 0, BATCH):
                        b, r = i + k, k % RING
                        dve.wait_ge(e_score, b + 1)
                        dve.tensor_tensor(slot(b, 0, 2 * DIM), ps[r][:], smax[:], ALU.subtract).then_inc(e_diff, 1)
                    if live(i, k, LAG2, BATCH):
                        b = i + k - LAG2
                        dve.wait_ge(e_exp, b + 1)
                        if not (phase == "head" and k == LAG2):
                            dve.wait_ge(e_sumv, b)
                        dve.tensor_tensor(ssum[:, ON_POOL:], slot(b, ON_POOL, 2 * DIM - ON_POOL), ssum[:, ON_POOL:], ALU.add).then_inc(e_sumv, 1)
                pipeline(dve, BATCH, RING, RING, LAG2, body)
                dve.wait_ge(e_sumv, BATCH)
                dve.wait_ge(e_sump, BATCH)
                dve.reciprocal(ssum[:], ssum[:])

            @block.scalar
            def _(act):
                def body(i, k, phase):
                    b = i + k
                    act.wait_ge(e_diff, b + 1)
                    act.activation(slot(b, 0, 2 * DIM), slot(b, 0, 2 * DIM), ACT.Exp, scale=SCORE_SCALE).then_inc(e_exp, 1)
                pipeline(act, BATCH, RING, RING, 0, body)

            @block.gpsimd
            def _(pool):
                def body(i, k, phase):
                    b = i + k
                    pool.wait_ge(e_exp, b + 1)
                    if not (phase == "head" and k == 0):
                        pool.wait_ge(e_sump, b)
                    pool.tensor_tensor(ssum[:, 0:ON_POOL], slot(b, 0, ON_POOL), ssum[:, 0:ON_POOL], ALU.add).then_inc(e_sump, 1)
                pipeline(pool, BATCH, RING, RING, 0, body)

        a_x_in = sems("a_x_in", RING)
        a_ctx_in = sems("a_ctx_in", RING)
        a_ctxTp = sem("a_ctxTp")
        a_ctxT = sem("a_ctxT")
        a_probv = sem("a_probv")
        a_probp = sem("a_probp")
        a_pv = sem("a_pv")
        a_x2 = sem("a_x2")
        a_stat = sem("a_stat")
        a_mean = sem("a_mean")
        a_pstep = sem("a_pstep")
        a_norm = sem("a_norm")
        a_xn = sem("a_xn")
        a_high = sem("a_high")
        a_low = sem("a_low")
        a_xnTp = sem("a_xnTp")
        a_xnT = sem("a_xnT")
        a_logit = sem("a_logit")
        a_top = sem("a_top")
        a_gap = sem("a_gap")
        a_egap = sem("a_egap")
        a_pd = sem("a_pd")
        a_p1 = sem("a_p1")
        a_p2 = sem("a_p2")
        a_stored = sems("a_stored", RING)
        L_PV, L_XN, L_T, L_LG, L_P = 1, 2, 3, 4, 4
        STORE_LAG = 8
        with nc.Block() as block:
            @block.sync
            def _(sp):
                def body(i, k, phase):
                    if live(i, k, 0, BATCH):
                        b, r = i + k, k % RING
                        if not (phase == "head" and k < RING):
                            sp.wait_ge(a_x2, b - RING + 1)
                        sp.dma_start(ring4k[:, r, :], ctx_rows[bass.ds(b * ROWS, ROWS), :]).then_inc(a_ctx_in[r], 16)
                        sp.dma_start(xring[:, r, :], x_rows[bass.ds(b * ROWS, ROWS), :]).then_inc(a_x_in[r], 16)
                    if live(i, k, STORE_LAG, BATCH):
                        b, r = i + k - STORE_LAG, k % RING
                        sp.wait_ge(a_p2, b + 1)
                        sp.wait_ge(a_low, b + 1)
                        if not (phase == "head" and k < STORE_LAG + RING):
                            sp.wait_ge(a_stored[r], 4 * b - 4 * r)
                        sp.dma_start(table[0][bass.ds(b * ROWS, ROWS), :], slot(b, 0, ROW)).then_inc(a_stored[r], 16)
                pipeline(sp, BATCH, RING, 3 * RING, STORE_LAG, body)
                for r in range(RING):
                    sp.wait_ge(a_stored[r], 16 * (BATCH // RING))

            @block.tensor
            def _(pe):
                def body(i, k, phase):
                    if live(i, k, 0, BATCH):
                        b, r = i + k, k % RING
                        pe.wait_ge(a_ctx_in[r], 4 * b + 16 - 4 * r)
                        if not (phase == "head" and k < 2):
                            pe.wait_ge(a_ctxT, b - 1)
                        for h in range(HC):
                            mm = pe.transpose(ps[k % 2][:, h * P:(h + 1) * P], ring4k[:, r, h * P:(h + 1) * P], ident[:])
                        mm.then_inc(a_ctxTp, 1)
                    if live(i, k, L_T, BATCH):
                        b, r = i + k - L_T, (k - L_T) % 2
                        pe.wait_ge(a_xn, b + 1)
                        if not (phase == "head" and k < L_T + 2):
                            pe.wait_ge(a_xnT, b - 1)
                        for h in range(HC):
                            mm = pe.transpose(ps[4 + r][:, h * P:(h + 1) * P], xn[:, r, h * P:(h + 1) * P], ident[:])
                        mm.then_inc(a_xnTp, 1)
                    if live(i, k, L_PV, BATCH):
                        b, r = i + k - L_PV, (k - L_PV) % 2
                        pe.wait_ge(a_ctxT, b + 1)
                        pe.wait_ge(a_probv, b + 1)
                        pe.wait_ge(a_probp, b + 1)
                        if not (phase == "head" and k < L_PV + 2):
                            pe.wait_ge(a_x2, b - 1)
                        for h in range(HC):
                            mm = pe.matmul(ps[2 + r][:, 0:DIM], ctxT[:, r, h * P:(h + 1) * P], slot(b, h * DIM, DIM), start=(h == 0), stop=(h == HC - 1))
                        mm.then_inc(a_pv, 1)
                    if live(i, k, L_LG, BATCH):
                        b, r = i + k - L_LG, (k - L_LG) % 2
                        pe.wait_ge(a_xnT, b + 1)
                        if not (phase == "head" and k < L_LG + 2):
                            pe.wait_ge(a_top, 2 * b - 2)
                        for h in range(HC):
                            mm = pe.matmul(ps[6 + r][:, 0:EXPERTS], xnT[:, r, h * P:(h + 1) * P], rwT[:, h, :], start=(h == 0), stop=(h == HC - 1))
                        mm.then_inc(a_logit, 1)
                pipeline(pe, BATCH, RING, 2 * RING, L_LG, body)

            @block.vector
            def _(dve):
                def body(i, k, phase):
                    if live(i, k, 0, BATCH):
                        b = i + k
                        dve.tensor_tensor(slot(b, ON_POOL, 2 * DIM - ON_POOL), slot(b, ON_POOL, 2 * DIM - ON_POOL), ssum[:, ON_POOL:], ALU.mult).then_inc(a_probv, 1)
                    if live(i, k, L_PV, BATCH):
                        b, r, r4 = i + k - L_PV, (k - L_PV) % 2, (k - L_PV) % RING
                        dve.wait_ge(a_pv, b + 1)
                        dve.wait_ge(a_x_in[r4], 4 * b + 16 - 4 * r4)
                        dve.tensor_tensor(slot(b, X2, DIM), ps[2 + r][:, 0:DIM], xring[:, r4, :], ALU.add).then_inc(a_x2, 1)
                    if live(i, k, L_T, BATCH):
                        b, r = i + k - L_T, (k - L_T) % 2
                        dve.wait_ge(a_high, b + 1)
                        dve.tensor_tensor(slot(b, P, P).bitcast(F16), xn[:, r, :], slot(b, 0, P).bitcast(F16), ALU.subtract).then_inc(a_low, 1)
                    if live(i, k, L_PV, BATCH):
                        b, r, r4 = i + k - L_PV, (k - L_PV) % 2, (k - L_PV) % RING
                        wait_apart(dve, a_x2, b + 1)
                        dve.bn_stats(stats[:, r4, :], slot(b, X2, DIM)).then_inc(a_stat, 1)
                    if live(i, k, L_P, BATCH):
                        b, r, r4 = i + k - L_P, (k - L_P) % 2, (k - L_P) % RING
                        wait_apart(dve, a_logit, b + 1)
                        dve.max(top[:, r4, :], ps[6 + r][:, 0:EXPERTS]).then_inc(a_top, 1)
                    if live(i, k, L_PV, BATCH):
                        b, r, r4 = i + k - L_PV, (k - L_PV) % 2, (k - L_PV) % RING
                        wait_apart(dve, a_stat, b + 1)
                        dve.bn_aggr(mv[:, r4, :], stats[:, r4, :]).then_inc(a_mean, 1)
                    if live(i, k, L_P, BATCH):
                        b, r, r4 = i + k - L_P, (k - L_P) % 2, (k - L_P) % RING
                        dve.wait_ge(a_top, 2 * b + 1)
                        dve.tensor_tensor(gap[:, r4:r4 + 1], top[:, r4, 1:2], top[:, r4, 0:1], ALU.subtract).then_inc(a_gap, 1)
                        dve.max_index(topi[:, r4, :], top[:, r4, :], ps[6 + r][:, 0:EXPERTS]).then_inc(a_top, 1)
                        dve.wait_ge(a_egap, b + 1)
                        dve.tensor_scalar(den[:, r4:r4 + 1], egap[:, r4:r4 + 1], WSCALE, WSCALE, ALU.mult, ALU.add).then_inc(a_pd, 1)
                        dve.wait_ge(a_top, 2 * b + 2)
                        for c in range(ROUNDS):
                            dve.tensor_copy(choice[:, c, bass.ds(b, 1)], topi[:, r4, c:c + 1])
                        dve.wait_ge(a_pd, b + 1)
                        dve.reciprocal(slot(b, PR, 1), den[:, r4:r4 + 1]).then_inc(a_p1, 1)
                        dve.wait_ge(a_p1, b + 1)
                        dve.tensor_scalar(slot(b, PR + 1, 1), slot(b, PR, 1), egap[:, r4:r4 + 1], None, ALU.mult).then_inc(a_p2, 1)
                pipeline(dve, BATCH, RING, 2 * RING, L_P, body)

            @block.gpsimd
            def _(pool):
                def body(i, k, phase):
                    if live(i, k, 0, BATCH):
                        b = i + k
                        pool.tensor_tensor(slot(b, 0, ON_POOL), slot(b, 0, ON_POOL), ssum[:, 0:ON_POOL], ALU.mult).then_inc(a_probp, 1)
                    if live(i, k, L_PV, BATCH):
                        b, r4 = i + k - L_PV, (k - L_PV) % RING
                        normalise_on_pool(pool, a_mean, b + 1, r4, a_norm, a_pstep, 2 * b)
                pipeline(pool, BATCH, RING, 2 * RING, L_PV, body)

            @block.scalar
            def _(act):
                def body(i, k, phase):
                    if live(i, k, 0, BATCH):
                        b = i + k
                        act.wait_ge(a_ctxTp, b + 1)
                        if not (phase == "head" and k < 2):
                            act.wait_ge(a_pv, b - 1)
                        act.activation(ctxT[:, k % 2, :], ps[k % 2][:, 0:DIM], ACT.Copy).then_inc(a_ctxT, 1)
                    if live(i, k, L_T, BATCH):
                        b, r = i + k - L_T, (k - L_T) % 2
                        act.wait_ge(a_xnTp, b + 1)
                        if not (phase == "head" and k < L_T + 2):
                            act.wait_ge(a_logit, b - 1)
                        act.activation(xnT[:, r, :], ps[4 + r][:, 0:DIM], ACT.Copy).then_inc(a_xnT, 1)
                    if live(i, k, L_P, BATCH):
                        b, r4 = i + k - L_P, (k - L_P) % RING
                        act.wait_ge(a_gap, b + 1)
                        act.activation(egap[:, r4:r4 + 1], gap[:, r4:r4 + 1], ACT.Exp).then_inc(a_egap, 1)
                    if live(i, k, L_XN, BATCH):
                        b, r, r4 = i + k - L_XN, (k - L_XN) % 2, (k - L_XN) % RING
                        act.wait_ge(a_norm, b + 1)
                        if not (phase == "head" and k < L_XN + 2):
                            act.wait_ge(a_xnTp, b - 1)
                            act.wait_ge(a_low, b - 1)
                        act.activation(xn[:, r, :], slot(b, X2, DIM), ACT.Identity, bias=shift[:, r4:r4 + 1], scale=rstd[:, r4:r4 + 1]).then_inc(a_xn, 1)
                        act.activation(slot(b, 0, P).bitcast(F16), slot(b, X2, DIM), ACT.Identity, bias=shift[:, r4:r4 + 1], scale=rstd[:, r4:r4 + 1]).then_inc(a_high, 1)
                pipeline(act, BATCH, RING, 2 * RING, L_LG, body)

        class Area:
            at = 0

            @classmethod
            def take(cls, words, rows=P):
                cls.at += words
                assert cls.at <= BATCH * ROW
                return slots[0:rows, cls.at - words:cls.at]

        N_RBE = ROUNDS * BATCH * EXPERTS
        row_buf = [Area.take(ROW) for _ in range(RING * SUB)]
        onehot = Area.take(N_RBE // 2).bitcast(F16)
        totals = Area.take(8)[0:BATCH].bitcast(F16)
        spread = Area.take(N_RBE // 2)[0:BATCH].bitcast(F16)
        place = Area.take(N_RBE)
        count = Area.take(16)
        count_i = Area.take(16).bitcast(I32)
        blocks = Area.take(16)
        ends = Area.take(16)
        base = Area.take(16)
        where = Area.take(ROUNDS * BATCH)
        where_i = Area.take(ROUNDS * BATCH).bitcast(I32)
        part_i = Area.take(ROUNDS * BATCH).bitcast(I32)
        tile_of = Area.take(ROUNDS * BATCH)
        lane_of = Area.take(ROUNDS * BATCH)
        lane_hot = [Area.take(P // 2).bitcast(F16) for _ in range(RING)]
        tile_hot = [Area.take(TILES).bitcast(F16) for _ in range(RING)]
        token = Area.take(ROUNDS * TILES)
        token_b = Area.take(ROUNDS * TILES)
        empty = Area.take(ROUNDS * TILES)
        index = Area.take(ROUNDS * GROUPS * 2 * SUB).bitcast(I32)
        past = Area.take(ROUNDS * GROUPS * EXPERTS, 1)
        owner = Area.take(ROUNDS * GROUPS, 1)
        owner_i = Area.take(ROUNDS * GROUPS, 1).bitcast(I32)
        b2_in = Area.take(EXPERTS * DIM, 1)
        b2_parts = Area.take(EXPERTS * DIM // 2, 2).bitcast(F16)
        b2_low = Area.take(EXPERTS * DIM // 2, 1).bitcast(F16)
        ring_idx = Area.take(RING * 2 * SUB).bitcast(I32)
        ring_b1 = Area.take(RING * FC)
        xT = [Area.take(2 * HC * GROUP // 2).bitcast(F16) for _ in range(2)]
        act32 = [Area.take(FC * GROUP) for _ in range(2)]
        act16 = [[Area.take(FC * GROUP // 2).bitcast(F16) for _ in range(2)] for _ in range(2)]

        r_hot = sem("r_hot")
        r_tot = sem("r_tot")
        r_totc = sem("r_totc")
        r_spread = sem("r_spread")
        r_pos = sem("r_pos")
        r_v = sem("r_v")
        r_made = sem("r_made")
        r_list = sem("r_list")
        r_b2 = sem("r_b2")
        r_b2s = sem("r_b2s")
        L4 = 2
        with nc.Block() as block:
            @block.sync
            def _(sp):
                sp.dma_start(b2_in, b2.rearrange("e (o h) -> o (e h)", o=1)).then_inc(r_b2, 16)
                sp.wait_ge(r_b2s, 2)
                sp.dma_start(b2_parts[1:2, :], b2_low).then_inc(r_b2, 16)
                sp.wait_ge(r_b2, 32)

            @block.scalar
            def _(act):
                act.wait_ge(r_b2, 16)
                act.activation(b2_parts[0:1, :], b2_in, ACT.Copy, scale=WSCALE).then_inc(r_b2s, 1)

            @block.tensor
            def _(pe):
                pe.wait_ge(r_hot, 1)
                hot = onehot.rearrange("p (r b e) -> p r b e", r=ROUNDS, e=EXPERTS)
                for r in range(ROUNDS):
                    pe.matmul(ps[r][:], before[:], onehot[:, r * 512:(r + 1) * 512], start=True, stop=False)
                    for e in range(EXPERTS):
                        mm = pe.matmul(ps[2][0:BATCH, r * 8 + e:r * 8 + e + 1], hot[:, r, :, e], ones16[:, 0:1], start=True, stop=True)
                mm.then_inc(r_tot, 1)
                pe.wait_ge(r_spread, 1)
                for r in range(ROUNDS):
                    pe.matmul(ps[r][:], ones16[0:BATCH, :], spread[:, r * 512:(r + 1) * 512], start=False, stop=True)
                pe.matmul(ps[3][:, 0:16], ones16[0:BATCH, :], totals[:, 0:16], start=True, stop=True).then_inc(r_pos, 1)
                for r in range(ROUNDS):
                    def body(i, k, phase):
                        b = i + k
                        pe.wait_ge(r_made, r * BATCH + b + 1)
                        first, last = (phase == "head" and k == 0), (phase == "tail" and k == RING - 1)
                        pe.matmul(ps[4 + r][:, 0:2 * TILES], lane_hot[k % RING], tile_hot[k % RING], start=first, stop=last,
                                  skip_group_check=True).then_inc(r_list, 1)
                    for k in range(RING):
                        body(0, k, "head")
                    with pe.Fori(1, BATCH // RING - 1) as block4:
                        i = pe.snap(block4 * RING)
                        for k in range(RING):
                            body(i, k, "loop")
                    for k in range(RING):
                        body(BATCH - RING, k, "tail")

            @block.vector
            def _(dve):
                steps = [0]

                def chain(op):
                    steps[0] += 1
                    op.then_inc(r_v, 1)
                    dve.wait_ge(r_v, steps[0])

                hot = onehot.rearrange("p (r b e) -> p r b e", r=ROUNDS, e=EXPERTS)
                dve.tensor_tensor(hot, choice[:].unsqueeze(3).to_broadcast([P, ROUNDS, BATCH, EXPERTS]),
                                  iota_e[:].unsqueeze(1).unsqueeze(1).to_broadcast([P, ROUNDS, BATCH, EXPERTS]), ALU.is_equal).then_inc(r_hot, 1)
                dve.wait_ge(r_tot, 1)
                chain(dve.tensor_copy(totals[:, 0:16], ps[2][0:BATCH, 0:16]))
                dve.tensor_tensor(spread.rearrange("p (r b e) -> p r b e", r=ROUNDS, e=EXPERTS),
                                  totals[:, 0:16].rearrange("p (r e) -> p r e", r=ROUNDS).unsqueeze(2).to_broadcast([BATCH, ROUNDS, BATCH, EXPERTS]),
                                  before[0:BATCH, 0:BATCH].unsqueeze(1).unsqueeze(3).to_broadcast([BATCH, ROUNDS, BATCH, EXPERTS]),
                                  ALU.mult).then_inc(r_spread, 1)
                dve.wait_ge(r_b2, 16)
                dve.wait_ge(r_b2s, 1)
                dve.scalar_tensor_tensor(b2_low, b2_in, WSCALE, b2_parts[0:1, :], ALU.mult, ALU.subtract).then_inc(r_b2s, 1)
                dve.wait_ge(r_pos, 1)
                chain(dve.tensor_scalar(count_i, ps[3][:, 0:16], float(GROUP - 1), None, ALU.add))
                chain(dve.tensor_scalar(count_i, count_i, GROUP.bit_length() - 1, None, ALU.arith_shift_right))
                chain(dve.tensor_copy(blocks, count_i))
                blk = blocks.rearrange("p (r e) -> p r e", r=ROUNDS)
                end = ends.rearrange("p (r e) -> p r e", r=ROUNDS)
                chain(dve.tensor_copy(end[:, :, 0:1], blk[:, :, 0:1]))
                for e in range(1, EXPERTS):
                    chain(dve.tensor_tensor(end[:, :, e:e + 1], end[:, :, e - 1:e], blk[:, :, e:e + 1], ALU.add))
                chain(dve.tensor_tensor(base, ends, blocks, ALU.subtract))
                chain(dve.tensor_scalar(base, base, float(GROUP), None, ALU.mult))
                pl = place.rearrange("p (r b e) -> p r b e", r=ROUNDS, e=EXPERTS)
                for r in range(ROUNDS):
                    dve.tensor_tensor(pl[:, r], ps[r][:].rearrange("p (b e) -> p b e", e=EXPERTS),
                                      base[:, r * 8:r * 8 + 8].unsqueeze(1).to_broadcast([P, BATCH, EXPERTS]), ALU.add).then_inc(r_v, 1)
                steps[0] += 2
                dve.wait_ge(r_v, steps[0])
                chain(dve.tensor_tensor(place, place, onehot, ALU.mult))
                chain(dve.tensor_reduce(where, pl.rearrange("p r b e -> p (r b) e"), AX_X, ALU.add))
                chain(dve.tensor_copy(where_i, where))
                chain(dve.tensor_scalar(part_i, where_i, 7, None, ALU.arith_shift_right))
                chain(dve.tensor_copy(tile_of, part_i))
                chain(dve.tensor_scalar(part_i, where_i, P - 1, None, ALU.bitwise_and))
                chain(dve.tensor_copy(lane_of, part_i))
                for r in range(ROUNDS):
                    def body(i, k, phase):
                        b = i + k
                        if not (phase == "head" and k < RING and r == 0):
                            dve.wait_ge(r_list, r * BATCH + b - RING + 1)
                        col = slice_of(r * BATCH + b)
                        dve.tensor_scalar(lane_hot[k % RING], iota16[:], lane_of[:, col], None, ALU.is_equal)
                        dve.tensor_scalar(tile_hot[k % RING][:, 0:TILES], iota16[:, 0:TILES], tile_of[:, col], iota_b1[:, slice_of(b)], ALU.is_equal, ALU.mult)
                        dve.tensor_scalar(tile_hot[k % RING][:, TILES:2 * TILES], iota16[:, 0:TILES], tile_of[:, col], row_no1[:], ALU.is_equal, ALU.mult).then_inc(r_made, 1)
                    pipeline(dve, BATCH, RING, RING, 0, body)
                dve.wait_ge(r_list, ROUNDS * BATCH)
                for r in range(ROUNDS):
                    dve.tensor_copy(token_b[:, r * TILES:(r + 1) * TILES], ps[4 + r][:, 0:TILES]).then_inc(r_v, 1)
                steps[0] += 2
                dve.wait_ge(r_v, steps[0])
                for r in range(ROUNDS):
                    dve.scalar_tensor_tensor(token[:, r * TILES:(r + 1) * TILES], token_b[:, r * TILES:(r + 1) * TILES], float(ROWS),
                                             ps[4 + r][:, TILES:2 * TILES], ALU.mult, ALU.add).then_inc(r_v, 1)
                steps[0] += 2
                dve.wait_ge(r_v, steps[0])
                ix = index.rearrange("p (n w s) -> p n w s", w=2, s=SUB)
                tk = token.rearrange("p (n s) -> p n s", s=SUB)
                chain(dve.tensor_scalar(empty, token, 0.0, float(SKIPPED), ALU.is_equal, ALU.mult))
                chain(dve.tensor_scalar(token, token, -1.0, None, ALU.add))
                chain(dve.tensor_tensor(empty, empty, token, ALU.add))
                chain(dve.tensor_scalar(ix[:, :, 0, :], tk, 0.0, None, ALU.max))
                chain(dve.tensor_copy(ix[:, :, 1, :], empty.rearrange("p (n s) -> p n s", s=SUB)))
                pst = past.rearrange("p (r g e) -> p r g e", r=ROUNDS, e=EXPERTS)
                for r in range(ROUNDS):
                    chain(dve.tensor_tensor(pst[:, r], ends[0:1, r * 8:r * 8 + 8].unsqueeze(1).to_broadcast([1, GROUPS, EXPERTS]),
                                            iota_g[:].unsqueeze(2).to_broadcast([1, GROUPS, EXPERTS]), ALU.is_le))
                chain(dve.tensor_reduce(owner, past.rearrange("p (n e) -> p n e", e=EXPERTS), AX_X, ALU.add))
                chain(dve.tensor_scalar(owner_i, owner, float(EXPERTS - 1), None, ALU.min))

        L_TR, L_G1, L_G2 = 1, 2, 3
        for rnd in range(ROUNDS):
            target = table[1] if rnd == 0 else out_rows
            n = f"x{rnd}_"
            x_rows_in = sems(n + "rows_in", RING)
            x_out = sems(n + "out", RING)
            x_idx = sem(n + "idx")
            x_b1 = sem(n + "b1")
            x_tr = sem(n + "tr")
            x_xT = sem(n + "xT")
            x_hid = sem(n + "hid")
            x_act = sem(n + "act")
            x_high = sem(n + "high")
            x_low = sem(n + "low")
            x_y = sem(n + "y")
            x_sum = sem(n + "sum")
            with nc.Block() as block:
                @block.gpsimd
                def _(pool):
                    def body(i, k, phase):
                        if live(i, k, 0, GROUPS):
                            g, r = i + k, k % RING
                            if not (phase == "head" and k < RING):
                                wait_apart(pool, x_out[r], 32 * (g // RING) if isinstance(g, int) else 8 * g - 8 * r)
                            pool.tensor_copy(ring_idx[:, r * 4:r * 4 + 4], index[:, bass.ds((g + rnd * GROUPS) * 4, 4)]).then_inc(x_idx, 1)
                            e = pool.value_load(owner_i[0:1, bass.ds(g + rnd * GROUPS, 1)], min_val=0, max_val=EXPERTS - 1)
                            pool.tensor_copy(ring_b1[:, r * FC:(r + 1) * FC], b1T[:].rearrange("p e f -> p (e f)")[:, bass.ds(e * FC, FC)]).then_inc(x_b1, 1)
                            wait_apart(pool, x_idx, g + 1)
                            for s in range(SUB):
                                pool.indirect_dma_start(row_buf[r * SUB + s], None, table[rnd],
                                                        bass.IndirectOffsetOnAxis(ap=ring_idx[:, r * 4 + s:r * 4 + s + 1], axis=0)).then_inc(x_rows_in[r], 16)
                        if live(i, k, L_G2, GROUPS):
                            g, r = i + k - L_G2, (k - L_G2) % RING
                            wait_apart(pool, x_sum, 2 * g + 2)
                            for s in range(SUB):
                                rows = row_buf[r * SUB + s] if rnd == 0 else row_buf[r * SUB + s][:, X2:X2 + DIM]
                                pool.indirect_dma_start(target, bass.IndirectOffsetOnAxis(ap=ring_idx[:, r * 4 + 2 + s:r * 4 + 3 + s], axis=0), rows, None,
                                                        bounds_check=TOKENS - 1, oob_is_err=False).then_inc(x_out[r], 16)
                    pipeline(pool, GROUPS, RING, RING, L_G2, body)
                    for r in range(RING):
                        pool.wait_ge(x_out[r], 32 * len(range(r, GROUPS, RING)))

                @block.tensor
                def _(pe):
                    def body(i, k, phase):
                        if live(i, k, L_TR, GROUPS):
                            g, r, r2 = i + k - L_TR, (k - L_TR) % RING, (k - L_TR) % 2
                            pe.wait_ge(x_rows_in[r], 32 * (g // RING + 1) if isinstance(g, int) else 8 * g + 32 - 8 * r)
                            if not (phase == "head" and k < L_TR + 2):
                                pe.wait_ge(x_xT, g - 1)
                            bank = ps[r2][:].bitcast(F16)
                            for c in range(2 * HC):
                                for s in range(SUB):
                                    mm = pe.transpose(bank[:, (c * SUB + s) * P:(c * SUB + s + 1) * P],
                                                      row_buf[r * SUB + s].bitcast(F16)[:, c * P:(c + 1) * P], ident16[:])
                            mm.then_inc(x_tr, 1)
                        if live(i, k, L_G2, GROUPS):
                            g, r2 = i + k - L_G2, (k - L_G2) % 2
                            e = pe.value_load(owner_i[0:1, bass.ds(g + rnd * GROUPS, 1)], min_val=0, max_val=EXPERTS - 1)
                            pe.wait_ge(x_low, 2 * g + 2)
                            if not (phase == "head" and k < L_G2 + 2):
                                pe.wait_ge(x_sum, 2 * g - 2)
                            for s in range(SUB):
                                y = ps[6 + r2][:, s * DIM:(s + 1) * DIM]
                                pe.matmul(y, ones16[0:2, :], b2_parts[:, bass.ds(e * DIM, DIM)], start=True, stop=False)
                                for f in range(FC):
                                    for pa, pw in ((0, 0), (1, 0), (0, 1)):
                                        mm = pe.matmul(y, act16[r2][pa][:, f * GROUP + s * P:f * GROUP + (s + 1) * P],
                                                       w2T[f][pw][:, bass.ds(e * DIM, DIM)], start=False, stop=(f == FC - 1 and pw == 1))
                                mm.then_inc(x_y, 1)
                        if live(i, k, L_G1, GROUPS):
                            g, r2 = i + k - L_G1, (k - L_G1) % 2
                            e = pe.value_load(owner_i[0:1, bass.ds(g + rnd * GROUPS, 1)], min_val=0, max_val=EXPERTS - 1)
                            pe.wait_ge(x_xT, g + 1)
                            if not (phase == "head" and k < L_G1 + 2):
                                pe.wait_ge(x_act, 4 * g - 4)
                            for f in range(FC):
                                h = ps[2 + 2 * r2 + f // 2][:, (f % 2) * GROUP:(f % 2 + 1) * GROUP]
                                for c in range(HC):
                                    for px, pw in ((0, 0), (1, 0), (0, 1)):
                                        mm = pe.matmul(h, w1T[c][f][pw][:, bass.ds(e * P, P)], xT[r2][:, (px * HC + c) * GROUP:(px * HC + c + 1) * GROUP],
                                                       start=(c == 0 and px == 0 and pw == 0), stop=(c == HC - 1 and pw == 1))
                                mm.then_inc(x_hid, 1)
                    pipeline(pe, GROUPS, RING, RING, L_G2, body)

                @block.scalar
                def _(act):
                    def body(i, k, phase):
                        if live(i, k, L_TR, GROUPS):
                            g, r2 = i + k - L_TR, (k - L_TR) % 2
                            act.wait_ge(x_tr, g + 1)
                            if not (phase == "head" and k < L_TR + 2):
                                act.wait_ge(x_hid, 4 * g - 4)
                            act.activation(xT[r2], ps[r2][:].bitcast(F16), ACT.Copy).then_inc(x_xT, 1)
                        if live(i, k, L_G1, GROUPS):
                            g, r, r2 = i + k - L_G1, (k - L_G1) % RING, (k - L_G1) % 2
                            act.wait_ge(x_b1, g + 1)
                            if not (phase == "head" and k < L_G1 + 2):
                                act.wait_ge(x_low, 2 * g - 2)
                            for f in range(FC):
                                act.wait_ge(x_hid, 4 * g + 2 * (f // 2) + 2)
                                act.activation(act32[r2][:, f * GROUP:(f + 1) * GROUP], ps[2 + 2 * r2 + f // 2][:, (f % 2) * GROUP:(f % 2 + 1) * GROUP],
                                               ACT.Gelu, bias=ring_b1[:, r * FC + f:r * FC + f + 1], scale=1.0 / WSCALE).then_inc(x_act, 1)
                    pipeline(act, GROUPS, RING, RING, L_G1, body)

                @block.vector
                def _(dve):
                    def body(i, k, phase):
                        if live(i, k, L_G2, GROUPS):
                            g, r, r2 = i + k - L_G2, (k - L_G2) % RING, (k - L_G2) % 2
                            dve.wait_ge(x_y, 2 * g + 2)
                            for s in range(SUB):
                                rows = row_buf[r * SUB + s]
                                dve.scalar_tensor_tensor(rows[:, X2:X2 + DIM], ps[6 + r2][:, s * DIM:(s + 1) * DIM], rows[:, PR + rnd:PR + rnd + 1],
                                                         rows[:, X2:X2 + DIM], ALU.mult, ALU.add).then_inc(x_sum, 1)
                        if live(i, k, L_G1, GROUPS):
                            g, r2 = i + k - L_G1, (k - L_G1) % 2
                            if not (phase == "head" and k < L_G1 + 2):
                                dve.wait_ge(x_y, 2 * g - 2)
                            for j in range(2):
                                dve.wait_ge(x_act, 4 * g + 2 * j + 2)
                                cols = slice(j * 2 * GROUP, (j + 1) * 2 * GROUP)
                                dve.tensor_copy(act16[r2][0][:, cols], act32[r2][:, cols]).then_inc(x_high, 1)
                                dve.wait_ge(x_high, 2 * g + j + 1)
                                dve.tensor_tensor(act16[r2][1][:, cols], act32[r2][:, cols], act16[r2][0][:, cols], ALU.subtract).then_inc(x_low, 1)
                    pipeline(dve, GROUPS, RING, RING, L_G2, body)


def slice_of(c):
    return bass.ds(c, 1)


_INS = ["x", "ctx_1024", "L0_ffn_router_w", "L0_ffn_w1", "L0_ffn_b1", "L0_ffn_w2", "L0_ffn_b2"]


def kernel(**inputs):
    import numpy as np
    import concourse.bacc as bacc
    from concourse.bass_utils import run_bass_kernel_spmd

    nc = bacc.Bacc("TRN2", target_bir_lowering=False, num_devices=1, dynamic_dma_scratch_size=8192)
    arrays, args = {}, []
    for name in _INS:
        a = np.ascontiguousarray(inputs[name])
        arrays[f"in_{name}"] = a
        args.append(nc.dram_tensor(f"in_{name}", a.shape, mybir.dt.from_np(a.dtype), kind="ExternalInput").ap())
    args.append(nc.dram_tensor("out_x", (BATCH, ROWS, DIM), F32, kind="ExternalOutput").ap())
    xattn_ffn(nc, *args)
    return run_bass_kernel_spmd(nc, [arrays], core_ids=[0]).results[0]["out_x"]
```

```python
from contextlib import ExitStack

import concourse.bass as bass
from concourse import mybir

F32 = mybir.dt.float32
F16 = mybir.dt.float16
I32 = mybir.dt.int32
U32 = mybir.dt.uint32
ALU = mybir.AluOpType
ACT = mybir.ActivationFunctionType
AX_X = mybir.AxisListType.X

P = 128
BATCH, ROWS, DIM = 64, 128, 256
EXPERTS, HID = 8, 512
TOKENS = BATCH * ROWS
HC = DIM // P
FC = HID // P
GROUP = 256
SUB = GROUP // P
GROUPS = TOKENS // GROUP + EXPERTS - 1
TILES = GROUPS * SUB
ROUNDS = 2
WSCALE = 64.0
SCORE_SCALE = 1.0 / 16.0
LN_EPS = 1e-5
ROW = 2 * DIM + 2
X2 = DIM
PR = 2 * DIM
SUM_DVE = 80
PROD_POOL = 240
SKIPPED = 16384
PAIRS = BATCH // 2
RING = 4
LANES = 6


def pipeline(eng, count, unroll, peel, last_lag, body):
    for k in range(peel):
        body(0, k, 0)
    whole = peel + (count - peel) // unroll * unroll
    if whole > peel:
        with eng.Fori(peel // unroll, whole // unroll) as block:
            i = eng.snap(block * unroll)
            for k in range(unroll):
                body(i, k, block)
    for k in range(count - whole + last_lag):
        body(whole, k, whole // unroll)


def live(i, k, lag, count):
    return not isinstance(i, int) or 0 <= i + k - lag < count


def after(eng, sem, count):
    if not isinstance(count, int) or count > 0:
        eng.wait_ge(sem, count)


def wait_apart(eng, sem, count):
    if not isinstance(count, int):
        eng.lower_val(count)
    eng.wait_ge(sem, 1)
    eng.wait_ge(sem, count)


def landed(n, ring):
    return 16 * (n // ring + 1)


def landed_at(i, k, ring):
    return i * (16 // ring) + landed(k, ring)


def xattn_ffn(nc, x, ctx, router_w, w1, b1, w2, b2, out):
    w1_rows = w1.rearrange("e f h -> (e f) h")
    w2_rows = w2.rearrange("e h f -> (e h) f")
    out_rows = out.rearrange("b c l -> (b c) l")
    table = [nc.dram_tensor("rows_first", [TOKENS, ROW], F32, kind="Internal").ap(),
             nc.dram_tensor("rows_second", [TOKENS, ROW], F32, kind="Internal").ap()]
    table_b = table[0].rearrange("(b c) w -> b c w", c=ROWS)

    with ExitStack() as stack:
        def sb(name, shape, dt=F32):
            return stack.enter_context(nc.sbuf_tensor(name, shape, dt))

        def sem(name):
            return stack.enter_context(nc.semaphore(name))

        def sems(name, n):
            return [sem(f"{name}{i}") for i in range(n)]

        slots = sb("slots", [P, BATCH * ROW])
        slots3 = slots[:].rearrange("p (b w) -> p b w", w=ROW)
        w1T = [[[sb(f"w1T_{h}_{f}_{p}", [P, EXPERTS * P], F16) for p in range(2)] for f in range(FC)] for h in range(HC)]
        w2T = [[sb(f"w2T_{f}_{p}", [P, EXPERTS * DIM], F16) for p in range(2)] for f in range(FC)]
        smax = sb("smax", [P, 2, 2 * DIM])
        ssum = smax[:, 1, :]
        work = sb("work", [P, 18, DIM])
        ctx_ring = work[:, 0:8, :]
        stage = work[:, 8:16, :]
        a_ctx = work[:, 0:4, :]
        a_x = work[:, 4:8, :]
        a_xnr = work[:, 8:12, :]
        a_ctxT = work[:, 12:16, :]
        a_xnT = work[:, 16:18, :]
        ident = sb("ident", [P, P])
        ident16 = sb("ident16", [P, P], F16)
        before = sb("before", [P, P], F16)
        ones16 = sb("ones16", [P, P], F16)
        iota16 = sb("iota16", [P, P], F16)
        iota_e = sb("iota_e", [P, EXPERTS])
        iota_g = sb("iota_g", [1, GROUPS])
        row_no1 = sb("row_no1", [P, 1])
        neg_half = sb("neg_half", [P, 2])
        rwT = sb("rwT", [P, HC, EXPERTS])
        b1T = sb("b1T", [P, EXPERTS, FC])
        rw_in = sb("rw_in", [EXPERTS, DIM])
        stats = sb("stats", [P, RING, 2, 6])
        mv = sb("mv", [P, RING, 2, 2])
        veps = sb("veps", [P, RING, 2])
        minus = sb("minus", [P, RING, 2])
        rstd = sb("rstd", [P, RING, 2])
        shift = sb("shift", [P, RING, 2])
        top = sb("top", [P, 2, 2, 8])
        topi = sb("topi", [P, 2, 2, 8], U32)
        warm = sb("warm", [P, 1])
        gap = sb("gap", [P, 2, 2])
        egap = sb("egap", [P, 2, 2])
        den = sb("den", [P, 2, 2])
        choice = sb("choice", [P, ROUNDS, BATCH])
        psum = stack.enter_context(nc.psum_tensor("psum", [P, 8, 512], F32))

        def slot(b, first, n):
            return slots[:, bass.ds(b * ROW + first, n)]

        def slot2(b, first, n):
            return slots3[:, bass.ds(b, 2), first:first + n]

        def pair_of(dram, b):
            return dram[bass.ds(b, 2), :, :].rearrange("b c l -> c b l")

        s_zero = sem("s_zero")
        s_const = sem("s_const")
        s_rw_in = sem("s_rw_in")
        s_b1_in = sem("s_b1_in")
        s_setT = sem("s_setT")
        s_setc = sem("s_setc")
        m_x_in = sems("m_x_in", RING)
        m_ctx_in = sems("m_ctx_in", RING)
        m_stat = sem("m_stat")
        m_mean = sem("m_mean")
        m_pstep = sem("m_pstep")
        m_norm = sem("m_norm")
        m_q = sem("m_q")
        m_score = sem("m_score")
        m_max = sem("m_max")
        m_top = sem("m_top")
        e_w_in = sems("e_w_in", 2)
        e_wT = sem("e_wT")
        e_whigh = sem("e_whigh")
        e_wlow = sem("e_wlow")
        e_diff = sem("e_diff")
        e_exp = sem("e_exp")
        e_sumv = sem("e_sumv")
        e_sump = sem("e_sump")
        e_recip = sem("e_recip")
        a_x_in = sems("a_x_in", 2)
        a_ctx_in = sems("a_ctx_in", 2)
        a_ctxTp = sem("a_ctxTp")
        a_ctxTs = sem("a_ctxTs")
        a_probv = sem("a_probv")
        a_probp = sem("a_probp")
        a_pv = sem("a_pv")
        a_x2 = sem("a_x2")
        a_stat = sem("a_stat")
        a_mean = sem("a_mean")
        a_pstep = sem("a_pstep")
        a_norm = sem("a_norm")
        a_xn = sem("a_xn")
        a_high = sem("a_high")
        a_low = sem("a_low")
        a_xnTp = sem("a_xnTp")
        a_xnTs = sem("a_xnTs")
        a_logit = sem("a_logit")
        a_top = sem("a_top")
        a_topi = sem("a_topi")
        a_gap = sem("a_gap")
        a_egap = sem("a_egap")
        a_den = sem("a_den")
        a_p1 = sem("a_p1")
        a_p2 = sem("a_p2")
        a_choice = sem("a_choice")
        a_stored = sems("a_stored", RING)
        r_hot = sem("r_hot")
        r_tot = sem("r_tot")
        r_spread = sem("r_spread")
        r_pos = sem("r_pos")
        r_v = sem("r_v")
        r_places = sem("r_places")
        r_ones = sem("r_ones")
        r_tiles = sem("r_tiles")
        r_rowno = sem("r_rowno")
        r_lane = sem("r_lane")
        r_list = sem("r_list")
        r_index = sem("r_index")
        r_owner = sem("r_owner")
        r_b2 = sem("r_b2")
        r_b2s = sem("r_b2s")

        taken = [0]

        def take(words, rows=P):
            taken[0] += words
            return slots[0:rows, taken[0] - words:taken[0]]

        N_RBE = ROUNDS * BATCH * EXPERTS
        onehot = take(N_RBE // 2).bitcast(F16)
        totals = take(8)[0:BATCH].bitcast(F16)
        spread = take(N_RBE // 2)[0:BATCH].bitcast(F16)
        place = take(N_RBE)
        count_i = take(16).bitcast(I32)
        blocks = take(16)
        ends = take(16)
        ends_half = take(16)
        base = take(16)
        where = take(ROUNDS * BATCH)
        where_i = take(ROUNDS * BATCH).bitcast(I32)
        tile_i = take(ROUNDS * BATCH).bitcast(I32)
        lane_i = take(ROUNDS * BATCH).bitcast(I32)
        tile_of = take(ROUNDS * BATCH // 2).bitcast(F16)
        lane_of = take(ROUNDS * BATCH // 2).bitcast(F16)
        iota_b = take(BATCH // 2).bitcast(F16)
        lane_hot = take(BATCH * P // 2).bitcast(F16)
        tile_hot = take(BATCH * TILES).bitcast(F16)
        tile_one = take(BATCH * TILES // 2).bitcast(F16)
        token_b = take(TILES)
        token = take(TILES)
        empty = take(TILES)
        index = take(ROUNDS * GROUPS * 2 * SUB).bitcast(I32)
        past = take(ROUNDS * GROUPS * EXPERTS, 1)
        owner = take(ROUNDS * GROUPS, 1)
        owner_i = take(ROUNDS * GROUPS, 1).bitcast(I32)
        ring_idx = take(LANES * 2 * SUB).bitcast(I32)
        ring_b1 = take(LANES * FC)
        assert taken[0] <= 28 * 2 * ROW
        b2_in = take(EXPERTS * DIM)
        b2_all = take(EXPERTS * DIM)
        assert taken[0] <= 28 * 2 * ROW
        row_buf = [take(ROW) for _ in range(LANES * SUB)]
        act16 = [[take(FC * GROUP // 2).bitcast(F16) for _ in range(2)] for _ in range(2)]
        assert taken[0] <= BATCH * ROW
        flat = work[:].rearrange("p a b -> p (a b)")
        act32 = [flat[:, j * FC * GROUP:(j + 1) * FC * GROUP] for j in range(2)]
        xT = [flat[:, 2 * FC * GROUP + j * 512:2 * FC * GROUP + (j + 1) * 512].bitcast(F16) for j in range(2)]

        x_rows_in = [sems(f"x{r}_rows_in", LANES) for r in range(ROUNDS)]
        x_out = [sems(f"x{r}_out", LANES) for r in range(ROUNDS)]
        x_idx = [sem(f"x{r}_idx") for r in range(ROUNDS)]
        x_b1 = [sem(f"x{r}_b1") for r in range(ROUNDS)]
        x_tr = [sem(f"x{r}_tr") for r in range(ROUNDS)]
        x_xT = [sem(f"x{r}_xT") for r in range(ROUNDS)]
        x_hid = [sem(f"x{r}_hid") for r in range(ROUNDS)]
        x_act = [sem(f"x{r}_act") for r in range(ROUNDS)]
        x_high = [sem(f"x{r}_high") for r in range(ROUNDS)]
        x_low = [sem(f"x{r}_low") for r in range(ROUNDS)]
        x_y = [sem(f"x{r}_y") for r in range(ROUNDS)]
        x_bias = [sem(f"x{r}_bias") for r in range(ROUNDS)]
        x_sum = [sem(f"x{r}_sum") for r in range(ROUNDS)]

        def hot_lanes(dve, rnd, q):
            w = BATCH // 4
            dve.tensor_tensor(lane_hot[:, q * w * P:(q + 1) * w * P].rearrange("p (b l) -> p b l", l=P),
                              lane_of[:, rnd * BATCH + q * w:rnd * BATCH + (q + 1) * w].unsqueeze(2).to_broadcast([P, w, P]),
                              iota16[:].unsqueeze(1).to_broadcast([P, w, P]), ALU.is_equal).then_inc(r_lane, 1)

        L_CTX = 2
        L_MAX = 3
        L_SUM, L_LOW = 2, 2
        L_CT, L_PV, L_XN, L_LOWX, L_XNT, L_LG, L_P = 1, 2, 4, 5, 5, 6, 7
        L_XL, L_STORE = 1, 8
        L_TR, L_G1, L_G2 = 2, 3, 4

        block = stack.enter_context(nc.Block())

        @block.sync
        def _(sp):
            sp.dma_start(rw_in[:], router_w).then_inc(s_rw_in, 16)
            sp.dma_start(work[0:EXPERTS, 16:18, :].rearrange("e a b -> e (a b)"), b1).then_inc(s_b1_in, 16)

            def load_scores(i, k, n):
                if live(i, k, 0, PAIRS):
                    m, r = i + k, k % RING
                    after(sp, m_mean, m - RING + 1)
                    sp.dma_start(slot2(m * 2, 0, DIM), pair_of(x, m * 2)).then_inc(m_x_in[r], 16)
                if live(i, k, L_CTX, PAIRS):
                    m, r = i + k - L_CTX, (k - L_CTX) % RING
                    after(sp, m_score, m - RING + 1)
                    sp.dma_start(ctx_ring[:, 2 * r:2 * r + 2, :], pair_of(ctx, m * 2)).then_inc(m_ctx_in[r], 16)
            pipeline(sp, PAIRS, RING, 2 * RING, L_CTX, load_scores)

            def load_exps(i, k, n):
                m, r = i + k, k % RING
                sp.wait_ge(m_score, m + PAIRS - RING + 1)
                sp.dma_start(ctx_ring[:, 2 * r:2 * r + 2, :], pair_of(ctx, m * 2)).then_inc(m_ctx_in[r], 16)
                if k % 2 == 0:
                    j = (k // 2) % 2
                    after(sp, e_wT, n * 2 + k // 2 - 1)
                    sp.dma_start(stage[:, 4 * j:4 * j + 2, :], w1_rows[bass.ds(m * P, 2 * P), :].rearrange("(q p) h -> p q h", p=P)).then_inc(e_w_in[j], 16)
                    sp.dma_start(stage[:, 4 * j + 2:4 * j + 4, :].rearrange("p a b -> p (a b)"), w2_rows[bass.ds(m * (P // 2), P), :]).then_inc(e_w_in[j], 16)
            pipeline(sp, PAIRS, RING, RING, 0, load_exps)

            def attend(i, k, n):
                if live(i, k, 0, PAIRS):
                    m, r = i + k, k % RING
                    if isinstance(i, int) and i + k < RING:
                        sp.wait_ge(m_score, 2 * PAIRS)
                        sp.wait_ge(e_wT, PAIRS // 2)
                    after(sp, a_ctxTp, m - 1)
                    sp.dma_start(a_ctx[:, 2 * (k % 2):2 * (k % 2) + 2, :], pair_of(ctx, m * 2)).then_inc(a_ctx_in[k % 2], 16)
                if live(i, k, L_XL, PAIRS):
                    m, r = i + k - L_XL, (k - L_XL) % 2
                    after(sp, a_x2, m - 1)
                    sp.dma_start(a_x[:, 2 * r:2 * r + 2, :], pair_of(x, m * 2)).then_inc(a_x_in[r], 16)
                if live(i, k, L_STORE, PAIRS):
                    m, r = i + k - L_STORE, (k - L_STORE) % RING
                    before_it = landed_at(i, k - L_STORE, RING) - 16
                    if not isinstance(i, int):
                        sp.lower_val(before_it)
                        sp.lower_val(m + 1)
                    sp.wait_ge(a_low, m + 1)
                    sp.wait_ge(a_p2, m + 1)
                    after(sp, a_stored[r], before_it)
                    sp.dma_start(table_b[bass.ds(m * 2, 2), :, :].rearrange("b c w -> c b w"), slot2(m * 2, 0, ROW)).then_inc(a_stored[r], 16)
            pipeline(sp, PAIRS, RING, 3 * RING, L_STORE, attend)

            for r in range(RING):
                sp.wait_ge(a_stored[r], 16 * 7)
            sp.dma_start(b2_in, b2.rearrange("e (o h) -> o (e h)", o=1).to_broadcast([P, EXPERTS * DIM])).then_inc(r_b2, 16)

        @block.gpsimd
        def _(pool):
            pool.memset(ident[:], 0.0).then_inc(s_zero, 1)
            pool.memset(ident16[:], 0.0).then_inc(s_zero, 1)
            pool.memset(before[:], 0.0).then_inc(s_zero, 1)
            pool.wait_ge(s_zero, 3)
            for mat in (ident, ident16):
                pool.affine_select(out=mat[:], in_=mat[:], pattern=[[-1, P]], compare_op=ALU.not_equal, fill=1.0,
                                   base=0, channel_multiplier=1)
            pool.affine_select(out=before[:], in_=before[:], pattern=[[-1, P]], compare_op=ALU.is_ge, fill=1.0,
                               base=0, channel_multiplier=1)
            pool.memset(neg_half[:], -0.5).then_inc(s_const, 1)

            def norm(ready, m, r, steps, done):
                wait_apart(pool, ready, m + 1)
                pool.tensor_scalar(veps[:, r, :], mv[:, r, :, 1], LN_EPS, None, ALU.add).then_inc(steps, 1)
                pool.tensor_scalar(minus[:, r, :], mv[:, r, :, 0], -1.0, None, ALU.mult).then_inc(steps, 1)
                pool.wait_ge(steps, m * 3 + 2)
                pool.tensor_tensor(rstd[:, r, :], veps[:, r, :], neg_half[:], ALU.pow).then_inc(steps, 1)
                pool.wait_ge(steps, m * 3 + 3)
                pool.tensor_tensor(shift[:, r, :], minus[:, r, :], rstd[:, r, :], ALU.mult).then_inc(done, 1)

            pipeline(pool, PAIRS, RING, RING, 0, lambda i, k, n: norm(m_mean, i + k, k % RING, m_pstep, m_norm))

            pool.memset(ones16[:], 1.0)
            pool.iota(iota16[:], [[1, P]], base=0, channel_multiplier=0, allow_small_or_imprecise_dtypes=True)
            pool.iota(iota_e[:], [[1, EXPERTS]], base=0, channel_multiplier=0, allow_small_or_imprecise_dtypes=True)
            pool.iota(iota_g[:], [[1, GROUPS]], base=0, channel_multiplier=0, allow_small_or_imprecise_dtypes=True)
            pool.iota(row_no1[:], [[0, 1]], base=1, channel_multiplier=1, allow_small_or_imprecise_dtypes=True).then_inc(s_const, 1)

            def add_up(i, k, n):
                for j in range(2):
                    b = (i + k) * 2 + j
                    if j == 0:
                        pool.wait_ge(e_exp, i + k + 1)
                    if isinstance(i, int) and i == 0 and k == 0 and j == 0:
                        pool.wait_ge(m_top, 1)
                        pool.tensor_copy(ssum[:, SUM_DVE:], slot(0, SUM_DVE, 2 * DIM - SUM_DVE)).then_inc(e_sump, 1)
                    else:
                        pool.wait_ge(e_sump, b)
                        pool.tensor_tensor(ssum[:, SUM_DVE:], slot(b, SUM_DVE, 2 * DIM - SUM_DVE), ssum[:, SUM_DVE:], ALU.add).then_inc(e_sump, 1)
            pipeline(pool, PAIRS, RING, RING, 0, add_up)

            pool.wait_ge(e_recip, 1)

            def attend(i, k, n):
                if live(i, k, 0, PAIRS):
                    m = i + k
                    pool.tensor_tensor(slot2(m * 2, 0, PROD_POOL), slot2(m * 2, 0, PROD_POOL),
                                       ssum[:, 0:PROD_POOL].unsqueeze(1).to_broadcast([P, 2, PROD_POOL]), ALU.mult).then_inc(a_probp, 1)
                if live(i, k, L_PV, PAIRS):
                    norm(a_mean, i + k - L_PV, (k - L_PV) % RING, a_pstep, a_norm)
            pipeline(pool, PAIRS, RING, 2 * RING, L_PV, attend)

            for r in range(RING):
                pool.wait_ge(a_stored[r], 16 * (PAIRS // RING))
            pool.wait_ge(r_owner, 1)
            for rnd in range(ROUNDS):
                target = table[1] if rnd == 0 else out_rows
                pool.wait_ge(r_index, rnd + 1)

                def group(i, k, n):
                    if live(i, k, 0, GROUPS):
                        g, r = i + k, k % LANES
                        after(pool, x_out[rnd][r], n * 32 + k // LANES * 32)
                        pool.tensor_copy(ring_idx[:, r * 4:r * 4 + 4], index[:, bass.ds((g + rnd * GROUPS) * 4, 4)]).then_inc(x_idx[rnd], 1)
                        pool.wait_ge(x_idx[rnd], 1)
                        e = pool.value_load(owner_i[0:1, bass.ds(g + rnd * GROUPS, 1)], min_val=0, max_val=EXPERTS - 1)
                        pool.tensor_copy(ring_b1[:, r * FC:(r + 1) * FC], b1T[:].rearrange("p e f -> p (e f)")[:, bass.ds(e * FC, FC)]).then_inc(x_b1[rnd], 1)
                        wait_apart(pool, x_idx[rnd], g + 1)
                        for s in range(SUB):
                            pool.indirect_dma_start(row_buf[r * SUB + s], None, table[rnd],
                                                    bass.IndirectOffsetOnAxis(ap=ring_idx[:, r * 4 + s:r * 4 + s + 1], axis=0)).then_inc(x_rows_in[rnd][r], 16)
                    if live(i, k, L_G2, GROUPS):
                        g, r = i + k - L_G2, (k - L_G2) % LANES
                        wait_apart(pool, x_sum[rnd], g + 1)
                        for s in range(SUB):
                            rows = row_buf[r * SUB + s] if rnd == 0 else row_buf[r * SUB + s][:, X2:X2 + DIM]
                            pool.indirect_dma_start(target, bass.IndirectOffsetOnAxis(ap=ring_idx[:, r * 4 + 2 + s:r * 4 + 3 + s], axis=0), rows, None,
                                                    bounds_check=TOKENS - 1, oob_is_err=False).then_inc(x_out[rnd][r], 16)
                pipeline(pool, GROUPS, LANES, LANES, L_G2, group)
                for r in range(LANES):
                    pool.wait_ge(x_out[rnd][r], 32 * len(range(r, GROUPS, LANES)))

        @block.tensor
        def _(pe):
            pe.wait_ge(s_const, 1)
            pe.wait_ge(s_rw_in, 16)
            for h in range(HC):
                mm = pe.transpose(psum[:, 6, h * 8:h * 8 + 8], rw_in[:, h * P:(h + 1) * P], ident[0:8, 0:8])
            pe.wait_ge(s_b1_in, 16)
            for f in range(FC):
                mm = pe.transpose(psum[:, 7, f * 8:f * 8 + 8], work[0:EXPERTS, 16 + f // 2, (f % 2) * P:(f % 2 + 1) * P], ident[0:8, 0:8])
            mm.then_inc(s_setT, 1)

            def score(b, r2, place, done):
                for h in range(HC):
                    mm = pe.matmul(psum[:, r2, h * DIM:(h + 1) * DIM], ctx_ring[:, place, h * P:(h + 1) * P], slot(b, 0, DIM), start=True, stop=True)
                if done:
                    mm.then_inc(m_score, 1)

            def scores_max(i, k, n):
                m, r = i + k, k % RING
                pe.wait_ge(m_ctx_in[r], landed_at(i, k, RING))
                after(pe, m_max, m - 1)
                for j in range(2):
                    pe.wait_ge(m_q, m * 2 + j + 1)
                    score(m * 2 + j, 2 * (k % 2) + j, 2 * r + j, j == 1)
            pipeline(pe, PAIRS, RING, RING, 0, scores_max)

            def scores_exp(i, k, n):
                m, r = i + k, k % RING
                pe.wait_ge(m_ctx_in[r], landed_at(i, k, RING) + 16 * (PAIRS // RING))
                if isinstance(i, int) and i == 0 and k < 2:
                    pe.wait_ge(m_max, PAIRS - 1 + k)
                after(pe, e_diff, m - 1)
                for j in range(2):
                    score(m * 2 + j, 2 * (k % 2) + j, 2 * r + j, j == 1)
                if k % 2 == 0:
                    j = (k // 2) % 2
                    pe.wait_ge(e_w_in[j], n * 32 + 32 * (k // 4) + 32)
                    if isinstance(i, int) and i == 0 and k == 0:
                        pe.wait_ge(s_setc, 1)
                    after(pe, e_wlow, n * 2 + k // 2 - 1)
                    for q in range(2):
                        for h in range(HC):
                            pe.transpose(psum[:, 4 + 2 * j, (q * HC + h) * P:(q * HC + h + 1) * P], stage[:, 4 * j + q, h * P:(h + 1) * P], ident[:])
                    for f in range(FC):
                        mm = pe.transpose(psum[:, 5 + 2 * j, f * P:(f + 1) * P], stage[:, 4 * j + 2 + f // 2, (f % 2) * P:(f % 2 + 1) * P], ident[:])
                    mm.then_inc(e_wT, 1)
            pipeline(pe, PAIRS, RING, RING, 0, scores_exp)

            def attend(i, k, n):
                if isinstance(i, int) and i == 0 and k == 0:
                    pe.wait_ge(e_diff, PAIRS)
                    pe.wait_ge(e_wlow, PAIRS // 2)
                if live(i, k, L_CT, PAIRS):
                    m, r = i + k - L_CT, (k - L_CT) % 2
                    pe.wait_ge(a_ctx_in[r], landed_at(i, k - L_CT, 2))
                    after(pe, a_ctxTs, m - 1)
                    for j in range(2):
                        for h in range(HC):
                            mm = pe.transpose(psum[:, r, (j * HC + h) * P:(j * HC + h + 1) * P], a_ctx[:, 2 * r + j, h * P:(h + 1) * P], ident[:])
                    mm.then_inc(a_ctxTp, 1)
                if live(i, k, L_XNT, PAIRS):
                    m, r = i + k - L_XNT, (k - L_XNT) % 2
                    pe.wait_ge(a_xn, m + 1)
                    after(pe, a_xnTs, m - 1)
                    for j in range(2):
                        for h in range(HC):
                            mm = pe.transpose(psum[:, 4 + r, (j * HC + h) * P:(j * HC + h + 1) * P], a_xnr[:, 2 * r + j, h * P:(h + 1) * P], ident[:])
                    mm.then_inc(a_xnTp, 1)
                if live(i, k, L_LG, PAIRS):
                    m, r = i + k - L_LG, (k - L_LG) % 2
                    pe.wait_ge(a_xnTs, m + 1)
                    after(pe, a_topi, m - 1)
                    for j in range(2):
                        for h in range(HC):
                            mm = pe.matmul(psum[:, 6 + r, j * 8:j * 8 + 8], a_xnT[:, j, h * P:(h + 1) * P], rwT[:, h, :], start=(h == 0), stop=(h == HC - 1))
                    mm.then_inc(a_logit, 1)
                if live(i, k, L_PV, PAIRS):
                    m, r = i + k - L_PV, (k - L_PV) % 2
                    pe.wait_ge(a_ctxTs, m + 1)
                    pe.wait_ge(a_probv, m + 1)
                    pe.wait_ge(a_probp, m + 1)
                    after(pe, a_x2, m - 1)
                    for j in range(2):
                        for h in range(HC):
                            mm = pe.matmul(psum[:, 2 + r, j * DIM:(j + 1) * DIM], a_ctxT[:, 2 * r + j, h * P:(h + 1) * P],
                                           slot(m * 2 + j, h * DIM, DIM), start=(h == 0), stop=(h == HC - 1))
                    mm.then_inc(a_pv, 1)
            pipeline(pe, PAIRS, RING, 2 * RING, L_LG, attend)

            pe.wait_ge(r_hot, 1)
            pe.wait_ge(a_x2, PAIRS)
            pe.wait_ge(s_const, 2)
            hot = onehot.rearrange("p (r b e) -> p r b e", r=ROUNDS, e=EXPERTS)
            for r in range(ROUNDS):
                pe.matmul(psum[:, r, :], before[:], onehot[:, r * 512:(r + 1) * 512], start=True, stop=False)
                for e in range(EXPERTS):
                    mm = pe.matmul(psum[0:BATCH, 2, r * 8 + e:r * 8 + e + 1], hot[:, r, :, e], ones16[:, 0:1], start=True, stop=True)
            mm.then_inc(r_tot, 1)
            pe.wait_ge(r_spread, 1)
            for r in range(ROUNDS):
                pe.matmul(psum[:, r, :], ones16[0:BATCH, :], spread[:, r * 512:(r + 1) * 512], start=False, stop=True)
            pe.matmul(psum[:, 3, 0:16], ones16[0:BATCH, :], totals[:, 0:16], start=True, stop=True).then_inc(r_pos, 1)

            def list_tokens(rnd):
                pe.wait_ge(r_tiles, rnd + 1)
                pe.wait_ge(r_rowno, rnd + 1)
                tiles = tile_hot.rearrange("p (n b) -> p n b", b=BATCH)
                for b in range(BATCH):
                    q = b // (BATCH // 4)
                    if b % (BATCH // 4) == 0:
                        pe.wait_ge(r_lane, 4 * rnd + q + 1)
                    mm = pe.matmul(psum[:, 1, 0:2 * TILES], lane_hot[:, b * P:(b + 1) * P], tiles[:, :, b], start=(b == 0), stop=(b == BATCH - 1))
                mm.then_inc(r_list, 1)

            list_tokens(0)

            for rnd in range(ROUNDS):
                def group(i, k, n):
                    if live(i, k, L_G1, GROUPS):
                        g, r2 = i + k - L_G1, (k - L_G1) % 2
                        e = pe.value_load(owner_i[0:1, bass.ds(g + rnd * GROUPS, 1)], min_val=0, max_val=EXPERTS - 1)
                        pe.wait_ge(x_xT[rnd], g + 1)
                        after(pe, x_act[rnd], g * 2 - 2)
                        for f in range(FC):
                            h = psum[:, 2 + 2 * r2 + f // 2, (f % 2) * GROUP:(f % 2 + 1) * GROUP]
                            for c in range(HC):
                                for px, pw in ((0, 0), (1, 0), (0, 1)):
                                    mm = pe.matmul(h, w1T[c][f][pw][:, bass.ds(e * P, P)], xT[r2][:, (px * HC + c) * GROUP:(px * HC + c + 1) * GROUP],
                                                   start=(c == 0 and px == 0 and pw == 0), stop=(c == HC - 1 and pw == 1))
                            if f % 2:
                                mm.then_inc(x_hid[rnd], 1)
                    if live(i, k, L_TR, GROUPS):
                        g, r = i + k - L_TR, (k - L_TR) % LANES
                        pe.wait_ge(x_rows_in[rnd][r], n * 32 + (k - L_TR) // LANES * 32 + 32)
                        after(pe, x_xT[rnd], g)
                        bank = psum[:, 0, :].bitcast(F16)
                        for c in range(2 * HC):
                            for s in range(SUB):
                                mm = pe.transpose(bank[:, (c * SUB + s) * P:(c * SUB + s + 1) * P],
                                                  row_buf[r * SUB + s].bitcast(F16)[:, c * P:(c + 1) * P], ident16[:])
                        mm.then_inc(x_tr[rnd], 1)
                    if live(i, k, L_G2, GROUPS):
                        g, r2 = i + k - L_G2, (k - L_G2) % 2
                        e = pe.value_load(owner_i[0:1, bass.ds(g + rnd * GROUPS, 1)], min_val=0, max_val=EXPERTS - 1)
                        pe.wait_ge(x_low[rnd], g * 2 + 2)
                        after(pe, x_sum[rnd], g - 1)
                        for s in range(SUB):
                            y = psum[:, 6 + r2, s * DIM:(s + 1) * DIM]
                            for f in range(FC):
                                for pa, pw in ((0, 0), (1, 0), (0, 1)):
                                    mm = pe.matmul(y, act16[r2][pa][:, f * GROUP + s * P:f * GROUP + (s + 1) * P],
                                                   w2T[f][pw][:, bass.ds(e * DIM, DIM)], start=(f == 0 and pa == 0 and pw == 0), stop=(f == FC - 1 and pw == 1))
                        mm.then_inc(x_y[rnd], 1)
                if rnd == 0:
                    pe.wait_ge(r_owner, 1)
                pipeline(pe, GROUPS, LANES, LANES, L_G2, group)
                if rnd == 0:
                    list_tokens(1)

        @block.vector
        def _(dve):
            dve.wait_ge(s_setT, 1)
            dve.tensor_copy(rwT[:].rearrange("p h e -> p (h e)"), psum[:, 6, 0:HC * 8])
            dve.tensor_copy(b1T[:].rearrange("p e f -> p f e"), psum[:, 7, 0:FC * 8].rearrange("p (f e) -> p f e", e=8)).then_inc(s_setc, 1)

            def maximum(i, k, n):
                if live(i, k, 0, PAIRS):
                    m, r = i + k, k % RING
                    wait_apart(dve, m_x_in[r], landed_at(i, k, RING))
                    for j in range(2):
                        dve.bn_stats(stats[:, r, j, :], slot(m * 2 + j, 0, DIM)).then_inc(m_stat, 1)
                if live(i, k, L_MAX, PAIRS):
                    m, r2 = i + k - L_MAX, (k - L_MAX) % 2
                    dve.wait_ge(m_score, m + 1)
                    banks = psum[:, 2 * r2:2 * r2 + 2, :]
                    if isinstance(m, int) and m == 0:
                        dve.tensor_copy(smax[:], banks).then_inc(m_max, 1)
                    else:
                        dve.wait_ge(m_max, m)
                        dve.tensor_tensor(smax[:], banks, smax[:], ALU.max).then_inc(m_max, 1)
                if live(i, k, 0, PAIRS):
                    m, r = i + k, k % RING
                    wait_apart(dve, m_stat, m * 2 + 2)
                    for j in range(2):
                        last = dve.bn_aggr(mv[:, r, j, :], stats[:, r, j, :])
                    last.then_inc(m_mean, 1)
            pipeline(dve, PAIRS, RING, RING, L_MAX, maximum)
            dve.wait_ge(m_max, PAIRS)
            dve.tensor_tensor(smax[:, 0, :], smax[:, 0, :], smax[:, 1, :], ALU.max).then_inc(m_top, 1)
            dve.wait_ge(m_top, 1)

            def add_up(m, j):
                if isinstance(m, int) and m == 0 and j == 0:
                    dve.tensor_copy(ssum[:, 0:SUM_DVE], slot(0, 0, SUM_DVE)).then_inc(e_sumv, 1)
                else:
                    dve.wait_ge(e_sumv, m * 2 + j)
                    dve.tensor_tensor(ssum[:, 0:SUM_DVE], slot(m * 2 + j, 0, SUM_DVE), ssum[:, 0:SUM_DVE], ALU.add).then_inc(e_sumv, 1)

            def exponentials(i, k, n):
                if live(i, k, L_SUM, PAIRS):
                    dve.wait_ge(e_exp, i + k - L_SUM + 1)
                    add_up(i + k - L_SUM, 0)
                if live(i, k, 0, PAIRS):
                    m, r2 = i + k, k % 2
                    dve.wait_ge(m_score, m + PAIRS + 1)
                    dve.tensor_tensor(slot2(m * 2, 0, 2 * DIM), psum[:, 2 * r2:2 * r2 + 2, :],
                                      smax[:, 0:1, :].to_broadcast([P, 2, 2 * DIM]), ALU.subtract).then_inc(e_diff, 1)
                if live(i, k, L_SUM, PAIRS):
                    add_up(i + k - L_SUM, 1)
                if k % 2 == 0 and live(i, k, L_LOW, PAIRS):
                    j = ((k - L_LOW) // 2) % 2
                    i0 = i + (k - L_LOW) // RING * RING
                    dve.wait_ge(e_whigh, n * 2 + (k - L_LOW) // 2 + 1)
                    for q in range(2):
                        for h in range(HC):
                            t = w1T[h][2 * j + q]
                            dve.scalar_tensor_tensor(t[1][:, bass.ds(i0 * (P // RING), P)], psum[:, 4 + 2 * j, (q * HC + h) * P:(q * HC + h + 1) * P], WSCALE,
                                                     t[0][:, bass.ds(i0 * (P // RING), P)], ALU.mult, ALU.subtract)
                    for f in range(FC):
                        at = bass.ds(i0 * (DIM // RING) + j * P, P)
                        last = dve.scalar_tensor_tensor(w2T[f][1][:, at], psum[:, 5 + 2 * j, f * P:(f + 1) * P], WSCALE, w2T[f][0][:, at], ALU.mult, ALU.subtract)
                    last.then_inc(e_wlow, 1)
            pipeline(dve, PAIRS, RING, RING, L_LOW, exponentials)
            dve.wait_ge(e_sumv, BATCH)
            dve.wait_ge(e_sump, BATCH)
            dve.reciprocal(ssum, ssum).then_inc(e_recip, 1)
            dve.wait_ge(e_recip, 1)

            def attend(i, k, n):
                if live(i, k, L_LOWX, PAIRS):
                    m, r = i + k - L_LOWX, (k - L_LOWX) % 2
                    dve.wait_ge(a_high, m + 1)
                    dve.tensor_tensor(slot2(m * 2, P, P).bitcast(F16), a_xnr[:, 2 * r:2 * r + 2, :], slot2(m * 2, 0, P).bitcast(F16), ALU.subtract).then_inc(a_low, 1)
                if live(i, k, L_P, PAIRS):
                    m, r2 = i + k - L_P, (k - L_P) % 2
                    dve.wait_ge(a_egap, m + 1)
                    dve.tensor_scalar(den[:, r2, :], egap[:, r2, :], WSCALE, WSCALE, ALU.mult, ALU.add).then_inc(a_den, 1)
                if live(i, k, L_LG, PAIRS):
                    m, r2 = i + k - L_LG, (k - L_LG) % 2
                    wait_apart(dve, a_logit, m + 1)
                    for j in range(2):
                        last = dve.max(top[:, r2, j, :], psum[:, 6 + r2, j * 8:j * 8 + 8])
                    last.then_inc(a_top, 1)
                if live(i, k, L_PV, PAIRS):
                    m, r = i + k - L_PV, (k - L_PV) % 2
                    dve.wait_ge(a_pv, m + 1)
                    dve.wait_ge(a_x_in[r], landed_at(i, k - L_PV, 2))
                    dve.tensor_tensor(slot2(m * 2, X2, DIM), psum[:, 2 + r, :].rearrange("p (b w) -> p b w", b=2), a_x[:, 2 * r:2 * r + 2, :], ALU.add).then_inc(a_x2, 1)
                if live(i, k, L_P, PAIRS):
                    m, r2 = i + k - L_P, (k - L_P) % 2
                    dve.wait_ge(a_den, m + 1)
                    dve.reciprocal(slot2(m * 2, PR, 1).rearrange("p b w -> p (b w)"), den[:, r2, :]).then_inc(a_p1, 1)
                if live(i, k, L_LG, PAIRS):
                    m, r2 = i + k - L_LG, (k - L_LG) % 2
                    wait_apart(dve, a_top, m + 1)
                    dve.tensor_tensor(gap[:, r2, :], top[:, r2, :, 1], top[:, r2, :, 0], ALU.subtract).then_inc(a_gap, 1)
                    for j in range(2):
                        last = dve.max_index(topi[:, r2, j, :], top[:, r2, j, :], psum[:, 6 + r2, j * 8:j * 8 + 8])
                    last.then_inc(a_topi, 1)
                if live(i, k, L_PV, PAIRS):
                    m, r4 = i + k - L_PV, (k - L_PV) % RING
                    wait_apart(dve, a_x2, m + 1)
                    for j in range(2):
                        last = dve.bn_stats(stats[:, r4, j, :], slot(m * 2 + j, X2, DIM))
                    last.then_inc(a_stat, 1)
                if live(i, k, L_P, PAIRS):
                    m, r2 = i + k - L_P, (k - L_P) % 2
                    dve.wait_ge(a_p1, m + 1)
                    dve.tensor_tensor(slot2(m * 2, PR + 1, 1).rearrange("p b w -> p (b w)"), slot2(m * 2, PR, 1).rearrange("p b w -> p (b w)"),
                                      egap[:, r2, :], ALU.mult).then_inc(a_p2, 1)
                if live(i, k, L_LG, PAIRS):
                    m, r2 = i + k - L_LG, (k - L_LG) % 2
                    dve.wait_ge(a_topi, m + 1)
                    dve.tensor_copy(choice[:, :, bass.ds(m * 2, 2)], topi[:, r2, :, 0:ROUNDS].rearrange("p b r -> p r b")).then_inc(a_choice, 1)
                if live(i, k, L_PV, PAIRS):
                    m, r4 = i + k - L_PV, (k - L_PV) % RING
                    wait_apart(dve, a_stat, m + 1)
                    for j in range(2):
                        last = dve.bn_aggr(mv[:, r4, j, :], stats[:, r4, j, :])
                    last.then_inc(a_mean, 1)
                if live(i, k, 0, PAIRS):
                    m = i + k
                    dve.tensor_tensor(slot2(m * 2, PROD_POOL, 2 * DIM - PROD_POOL), slot2(m * 2, PROD_POOL, 2 * DIM - PROD_POOL),
                                      ssum[:, PROD_POOL:].unsqueeze(1).to_broadcast([P, 2, 2 * DIM - PROD_POOL]), ALU.mult).then_inc(a_probv, 1)
            pipeline(dve, PAIRS, RING, 2 * RING, L_P, attend)

            steps = [0]

            def chain(*ops):
                steps[0] += len(ops)
                for op in ops:
                    op.then_inc(r_v, 1)
                dve.wait_ge(r_v, steps[0])

            for r in range(RING):
                dve.wait_ge(a_stored[r], 16 * 7)
            dve.wait_ge(s_const, 2)
            dve.wait_ge(a_choice, PAIRS)
            hot = onehot.rearrange("p (r b e) -> p r b e", r=ROUNDS, e=EXPERTS)
            dve.tensor_tensor(hot, choice[:].unsqueeze(3).to_broadcast([P, ROUNDS, BATCH, EXPERTS]),
                              iota_e[:].unsqueeze(1).unsqueeze(1).to_broadcast([P, ROUNDS, BATCH, EXPERTS]), ALU.is_equal).then_inc(r_hot, 1)
            dve.wait_ge(r_tot, 1)
            chain(dve.tensor_copy(totals[:, 0:16], psum[0:BATCH, 2, 0:16]))
            dve.tensor_tensor(spread.rearrange("p (r b e) -> p r b e", r=ROUNDS, e=EXPERTS),
                              totals[:, 0:16].rearrange("p (r e) -> p r e", r=ROUNDS).unsqueeze(2).to_broadcast([BATCH, ROUNDS, BATCH, EXPERTS]),
                              before[0:BATCH, 0:BATCH].unsqueeze(1).unsqueeze(3).to_broadcast([BATCH, ROUNDS, BATCH, EXPERTS]),
                              ALU.mult).then_inc(r_spread, 1)
            dve.tensor_copy(iota_b, iota16[:, 0:BATCH])
            dve.wait_ge(r_pos, 1)
            chain(dve.tensor_scalar(count_i, psum[:, 3, 0:16], float(GROUP - 1), None, ALU.add))
            chain(dve.tensor_scalar(count_i, count_i, GROUP.bit_length() - 1, None, ALU.arith_shift_right))
            chain(dve.tensor_copy(blocks, count_i))
            blk = blocks.rearrange("p (r e) -> p r e", r=ROUNDS)
            end = ends.rearrange("p (r e) -> p r e", r=ROUNDS)
            half_end = ends_half.rearrange("p (r e) -> p r e", r=ROUNDS)
            source, other = blk, [end, half_end]
            for far in (1, 2, 4):
                sums = other[far == 2]
                chain(dve.tensor_copy(sums[:, :, 0:far], source[:, :, 0:far]),
                      dve.tensor_tensor(sums[:, :, far:], source[:, :, far:], source[:, :, 0:EXPERTS - far], ALU.add))
                source = sums
            chain(dve.tensor_tensor(base, ends, blocks, ALU.subtract))
            chain(dve.tensor_scalar(base, base, float(GROUP), None, ALU.mult))
            pl = place.rearrange("p (r b e) -> p r b e", r=ROUNDS, e=EXPERTS)
            chain(*[dve.tensor_tensor(pl[:, r], psum[:, r, :].rearrange("p (b e) -> p b e", e=EXPERTS),
                                      base[:, r * 8:r * 8 + 8].unsqueeze(1).to_broadcast([P, BATCH, EXPERTS]), ALU.add) for r in range(ROUNDS)])
            chain(dve.tensor_tensor(place, place, onehot, ALU.mult))
            chain(dve.tensor_reduce(where, pl.rearrange("p r b e -> p (r b) e"), AX_X, ALU.add))
            chain(dve.tensor_copy(where_i, where))
            chain(dve.tensor_scalar(tile_i, where_i, 7, None, ALU.arith_shift_right),
                  dve.tensor_scalar(lane_i, where_i, P - 1, None, ALU.bitwise_and))
            dve.tensor_copy(tile_of, tile_i).then_inc(r_places, 1)
            dve.tensor_copy(lane_of, lane_i).then_inc(r_places, 1)

            def hot_tiles(rnd):
                dve.tensor_tensor(tile_one.rearrange("p (n b) -> p n b", b=BATCH),
                                  tile_of[:, rnd * BATCH:(rnd + 1) * BATCH].unsqueeze(1).to_broadcast([P, TILES, BATCH]),
                                  iota16[:, 0:TILES].unsqueeze(2).to_broadcast([P, TILES, BATCH]), ALU.is_equal).then_inc(r_ones, 1)

            def batch_tiles(rnd):
                dve.wait_ge(r_ones, rnd + 1)
                dve.tensor_tensor(tile_hot[:, 0:TILES * BATCH].rearrange("p (n b) -> p n b", b=BATCH), tile_one.rearrange("p (n b) -> p n b", b=BATCH),
                                  iota_b.unsqueeze(1).to_broadcast([P, TILES, BATCH]), ALU.mult).then_inc(r_tiles, 1)

            def indices(rnd):
                dve.wait_ge(r_list, rnd + 1)
                chain(dve.tensor_copy(token_b, psum[:, 1, 0:TILES]))
                chain(dve.scalar_tensor_tensor(token, token_b, float(ROWS), psum[:, 1, TILES:2 * TILES], ALU.mult, ALU.add))
                ix = index.rearrange("p (r n w s) -> p r n w s", r=ROUNDS, w=2, s=SUB)[:, rnd]
                chain(dve.tensor_scalar(empty, token, 0.0, float(SKIPPED), ALU.is_equal, ALU.mult),
                      dve.tensor_scalar(ix[:, :, 0, :], token.rearrange("p (n s) -> p n s", s=SUB), -1.0, 0.0, ALU.add, ALU.max))
                dve.scalar_tensor_tensor(ix[:, :, 1, :], token.rearrange("p (n s) -> p n s", s=SUB), -1.0, empty.rearrange("p (n s) -> p n s", s=SUB),
                                         ALU.add, ALU.add).then_inc(r_index, 1)

            dve.wait_ge(r_places, 2)
            hot_tiles(0)
            batch_tiles(0)
            for q in range(4):
                hot_lanes(dve, 0, q)
            pst = past.rearrange("p (r g e) -> p r g e", r=ROUNDS, e=EXPERTS)
            chain(*[dve.tensor_tensor(pst[:, r], ends[0:1, r * 8:r * 8 + 8].unsqueeze(1).to_broadcast([1, GROUPS, EXPERTS]),
                                      iota_g[:].unsqueeze(2).to_broadcast([1, GROUPS, EXPERTS]), ALU.is_le) for r in range(ROUNDS)])
            chain(dve.tensor_reduce(owner, past.rearrange("p (n e) -> p n e", e=EXPERTS), AX_X, ALU.add))
            dve.tensor_scalar(owner_i, owner, float(EXPERTS - 1), None, ALU.min).then_inc(r_owner, 1)
            indices(0)

            dve.wait_ge(r_b2s, 1)
            for rnd in range(ROUNDS):
                def group(i, k, n):
                    if live(i, k, L_G1, GROUPS):
                        g, r, r2 = i + k - L_G1, (k - L_G1) % LANES, (k - L_G1) % 2
                        after(dve, x_y[rnd], g - 1)
                        for j in range(2):
                            dve.wait_ge(x_act[rnd], g * 2 + j + 1)
                            cols = slice(j * 2 * GROUP, (j + 1) * 2 * GROUP)
                            dve.tensor_copy(act16[r2][0][:, cols], act32[r2][:, cols]).then_inc(x_high[rnd], 1)
                            dve.wait_ge(x_high[rnd], g * 2 + j + 1)
                            dve.tensor_tensor(act16[r2][1][:, cols], act32[r2][:, cols], act16[r2][0][:, cols], ALU.subtract).then_inc(x_low[rnd], 1)
                        e = dve.value_load(owner_i[0:1, bass.ds(g + rnd * GROUPS, 1)], min_val=0, max_val=EXPERTS - 1)
                        dve.wait_ge(x_rows_in[rnd][r], n * 32 + (k - L_G1) // LANES * 32 + 32)
                        for s in range(SUB):
                            rows = row_buf[r * SUB + s]
                            last = dve.scalar_tensor_tensor(rows[:, X2:X2 + DIM], b2_all[:, bass.ds(e * DIM, DIM)], rows[:, PR + rnd:PR + rnd + 1],
                                                            rows[:, X2:X2 + DIM], ALU.mult, ALU.add)
                        last.then_inc(x_bias[rnd], 1)
                    if live(i, k, L_G2, GROUPS):
                        g, r, r2 = i + k - L_G2, (k - L_G2) % LANES, (k - L_G2) % 2
                        dve.wait_ge(x_bias[rnd], g + 1)
                        dve.wait_ge(x_y[rnd], g + 1)
                        for s in range(SUB):
                            rows = row_buf[r * SUB + s]
                            last = dve.scalar_tensor_tensor(rows[:, X2:X2 + DIM], psum[:, 6 + r2, s * DIM:(s + 1) * DIM], rows[:, PR + rnd:PR + rnd + 1],
                                                            rows[:, X2:X2 + DIM], ALU.mult, ALU.add)
                        last.then_inc(x_sum[rnd], 1)
                    if rnd == 0 and isinstance(i, int) and i + k == 0:
                        dve.wait_ge(r_rowno, 1)
                        hot_tiles(1)
                    if rnd == 0 and isinstance(i, int) and i + k == 1:
                        dve.wait_ge(r_list, 1)
                        batch_tiles(1)
                    if rnd == 0 and isinstance(i, int) and 2 <= i + k < 6:
                        hot_lanes(dve, 1, i + k - 2)
                pipeline(dve, GROUPS, LANES, LANES, L_G2, group)
                if rnd == 0:
                    indices(1)

        @block.scalar
        def _(act):
            def queries(i, k, n):
                m, r = i + k, k % RING
                act.wait_ge(m_norm, m + 1)
                for j in range(2):
                    act.activation(slot(m * 2 + j, 0, DIM), slot(m * 2 + j, 0, DIM), ACT.Identity, bias=shift[:, r, j:j + 1],
                                   scale=rstd[:, r, j:j + 1]).then_inc(m_q, 1)
            pipeline(act, PAIRS, RING, RING, 0, queries)

            def exponentials(i, k, n):
                m = i + k
                act.wait_ge(e_diff, m + 1)
                act.activation(slot2(m * 2, 0, 2 * DIM), slot2(m * 2, 0, 2 * DIM), ACT.Exp, scale=SCORE_SCALE).then_inc(e_exp, 1)
                if k % 2 == 0:
                    j = (k // 2) % 2
                    i0 = i + k // RING * RING
                    act.wait_ge(e_wT, n * 2 + k // 2 + 1)
                    for q in range(2):
                        for h in range(HC):
                            act.activation(w1T[h][2 * j + q][0][:, bass.ds(i0 * (P // RING), P)], psum[:, 4 + 2 * j, (q * HC + h) * P:(q * HC + h + 1) * P],
                                           ACT.Copy, scale=WSCALE)
                    for f in range(FC):
                        last = act.activation(w2T[f][0][:, bass.ds(i0 * (DIM // RING) + j * P, P)], psum[:, 5 + 2 * j, f * P:(f + 1) * P], ACT.Copy, scale=WSCALE)
                    last.then_inc(e_whigh, 1)
            pipeline(act, PAIRS, RING, RING, 0, exponentials)

            def attend(i, k, n):
                if live(i, k, L_CT, PAIRS):
                    m, r = i + k - L_CT, (k - L_CT) % 2
                    act.wait_ge(a_ctxTp, m + 1)
                    after(act, a_pv, m - 1)
                    if isinstance(m, int) and m == 0:
                        act.wait_ge(e_wT, PAIRS // 2)
                    act.activation(a_ctxT[:, 2 * r:2 * r + 2, :].rearrange("p a b -> p (a b)"), psum[:, r, :], ACT.Copy).then_inc(a_ctxTs, 1)
                if live(i, k, L_XN, PAIRS):
                    m, r, r4 = i + k - L_XN, (k - L_XN) % 2, (k - L_XN) % RING
                    after(act, a_low, m - 1)
                    after(act, a_xnTp, m - 1)
                    act.wait_ge(a_norm, m + 1)
                    for j in range(2):
                        last = act.activation(a_xnr[:, 2 * r + j, :], slot(m * 2 + j, X2, DIM), ACT.Identity, bias=shift[:, r4, j:j + 1], scale=rstd[:, r4, j:j + 1])
                    last.then_inc(a_xn, 1)
                if live(i, k, L_XNT, PAIRS):
                    m, r = i + k - L_XNT, (k - L_XNT) % 2
                    act.wait_ge(a_xnTp, m + 1)
                    after(act, a_logit, m)
                    act.activation(a_xnT.rearrange("p a b -> p (a b)"), psum[:, 4 + r, :], ACT.Copy).then_inc(a_xnTs, 1)
                if live(i, k, L_XN, PAIRS):
                    m, r = i + k - L_XN, (k - L_XN) % 2
                    act.wait_ge(a_xn, m + 1)
                    act.activation(slot2(m * 2, 0, P).bitcast(F16), a_xnr[:, 2 * r:2 * r + 2, :], ACT.Copy).then_inc(a_high, 1)
                if live(i, k, L_LG, PAIRS):
                    m, r2 = i + k - L_LG, (k - L_LG) % 2
                    act.wait_ge(a_gap, m + 1)
                    act.activation(egap[:, r2, :], gap[:, r2, :], ACT.Exp).then_inc(a_egap, 1)
            pipeline(act, PAIRS, RING, 2 * RING, L_LG, attend)

            act.wait_ge(r_b2, 16)
            act.activation(b2_all, b2_in, ACT.Copy, scale=WSCALE).then_inc(r_b2s, 1)

            def row_numbers(rnd):
                act.wait_ge(r_ones, rnd + 1)
                act.activation(tile_hot[:, TILES * BATCH:], tile_one, ACT.Identity, scale=row_no1[:]).then_inc(r_rowno, 1)

            row_numbers(0)
            act.activation(warm[:], row_no1[:], ACT.Gelu)

            for rnd in range(ROUNDS):
                def group(i, k, n):
                    if live(i, k, L_G1, GROUPS):
                        g, r, r2 = i + k - L_G1, (k - L_G1) % LANES, (k - L_G1) % 2
                        act.wait_ge(x_b1[rnd], g + 1)
                        after(act, x_low[rnd], g * 2 - 2)
                        for f in range(FC):
                            if f % 2 == 0:
                                act.wait_ge(x_hid[rnd], g * 2 + f // 2 + 1)
                            last = act.activation(act32[r2][:, f * GROUP:(f + 1) * GROUP], psum[:, 2 + 2 * r2 + f // 2, (f % 2) * GROUP:(f % 2 + 1) * GROUP],
                                                  ACT.Gelu, bias=ring_b1[:, r * FC + f:r * FC + f + 1], scale=1.0 / WSCALE)
                            if f % 2:
                                last.then_inc(x_act[rnd], 1)
                    if live(i, k, L_TR, GROUPS):
                        g, r2 = i + k - L_TR, (k - L_TR) % 2
                        act.wait_ge(x_tr[rnd], g + 1)
                        after(act, x_hid[rnd], g * 2 - 2)
                        act.activation(xT[r2], psum[:, 0, :].bitcast(F16), ACT.Copy).then_inc(x_xT[rnd], 1)
                    if rnd == 0 and isinstance(i, int) and i + k == 4:
                        row_numbers(1)
                pipeline(act, GROUPS, LANES, LANES, L_G2, group)


_INS = ["x", "ctx_1024", "L0_ffn_router_w", "L0_ffn_w1", "L0_ffn_b1", "L0_ffn_w2", "L0_ffn_b2"]


def kernel(**inputs):
    import numpy as np
    import concourse.bacc as bacc
    from concourse.bass_utils import run_bass_kernel_spmd

    nc = bacc.Bacc("TRN2", target_bir_lowering=False, num_devices=1, dynamic_dma_scratch_size=4096)
    arrays, args = {}, []
    for name in _INS:
        a = np.ascontiguousarray(inputs[name])
        arrays[f"in_{name}"] = a
        args.append(nc.dram_tensor(f"in_{name}", a.shape, mybir.dt.from_np(a.dtype), kind="ExternalInput").ap())
    args.append(nc.dram_tensor("out_x", (BATCH, ROWS, DIM), F32, kind="ExternalOutput").ap())
    xattn_ffn(nc, *args)
    return run_bass_kernel_spmd(nc, [arrays], core_ids=[0]).results[0]["out_x"]
```

```python
from contextlib import ExitStack

import concourse.bass as bass
from concourse import mybir

F32 = mybir.dt.float32
F16 = mybir.dt.float16
I32 = mybir.dt.int32
U32 = mybir.dt.uint32
ALU = mybir.AluOpType
ACT = mybir.ActivationFunctionType
AX_X = mybir.AxisListType.X

P = 128
BATCH, ROWS, DIM = 64, 128, 256
EXPERTS, HID = 8, 512
TOKENS = BATCH * ROWS
HC = DIM // P
FC = HID // P
GROUP = 256
SUB = GROUP // P
GROUPS = TOKENS // GROUP + EXPERTS - 1
TILES = GROUPS * SUB
ROUNDS = 2
WSCALE = 64.0
SCORE_SCALE = 1.0 / 16.0
LN_EPS = 1e-5
ROW = 2 * DIM + 2
X2 = 0
XN = DIM
PR = 2 * DIM
SUM_DVE = 128
PROD_POOL = 320
SKIPPED = 16384
PAIRS = BATCH // 2
RING = 4
LANES = 6
L_TR, L_G1, L_G2 = 2, 3, 4


def pipeline(eng, count, unroll, peel, last_lag, body):
    for k in range(peel):
        body(0, k, 0)
    whole = peel + (count - peel) // unroll * unroll
    if whole > peel:
        with eng.Fori(peel // unroll, whole // unroll) as block:
            i = eng.snap(block * unroll)
            for k in range(unroll):
                body(i, k, block)
    for k in range(count - whole + last_lag):
        body(whole, k, whole // unroll)


def expert_steps(eng, body):
    whole = GROUPS // LANES
    resume = -(-(GROUPS + L_G2) // LANES)
    last = ROUNDS * GROUPS // LANES
    for k in range(LANES):
        body(0, k, 0, None)
    with eng.Fori(1, whole) as block:
        i = eng.snap(block * LANES)
        for k in range(LANES):
            body(i, k, block, 0)
    for k in range((resume - whole) * LANES):
        body(whole * LANES, k, whole, None)
    with eng.Fori(resume, last) as block:
        i = eng.snap(block * LANES)
        for k in range(LANES):
            body(i, k, block, 1)
    for k in range(ROUNDS * GROUPS - last * LANES + L_G2):
        body(last * LANES, k, last, None)


def round_of(i, k, lag, rnd):
    return (i + k - lag) // GROUPS if rnd is None else rnd


def live(i, k, lag, count):
    return not isinstance(i, int) or 0 <= i + k - lag < count


def after(eng, sem, count):
    if not isinstance(count, int) or count > 0:
        eng.wait_ge(sem, count)


def wait_apart(eng, sem, count):
    if not isinstance(count, int):
        eng.lower_val(count)
    eng.wait_ge(sem, 1)
    eng.wait_ge(sem, count)


def landed(n, ring):
    return 16 * (n // ring + 1)


def landed_at(i, k, ring):
    return i * (16 // ring) + landed(k, ring)


def xattn_ffn(nc, x, ctx, router_w, w1, b1, w2, b2, out):
    w1_rows = w1.rearrange("e f h -> (e f) h")
    w2_rows = w2.rearrange("e h f -> (e h) f")
    out_rows = out.rearrange("b c l -> (b c) l")
    table = [nc.dram_tensor("rows_first", [TOKENS, ROW], F32, kind="Internal").ap(),
             nc.dram_tensor("rows_second", [TOKENS, ROW], F32, kind="Internal").ap()]
    table_b = table[0].rearrange("(b c) w -> b c w", c=ROWS)

    with ExitStack() as stack:
        def sb(name, shape, dt=F32):
            return stack.enter_context(nc.sbuf_tensor(name, shape, dt))

        def sem(name):
            return stack.enter_context(nc.semaphore(name))

        def sems(name, n):
            return [sem(f"{name}{i}") for i in range(n)]

        slots = sb("slots", [P, BATCH * ROW])
        slots3 = slots[:].rearrange("p (b w) -> p b w", w=ROW)
        w1T = [sb(f"w1T_{p}", [P, FC, HC, EXPERTS * P], F16) for p in ("high", "low")]
        w2T = [sb(f"w2T_{p}", [P, FC, EXPERTS * DIM], F16) for p in ("high", "low")]
        smax = sb("smax", [P, 3, 2 * DIM])
        sums = smax[:, 1:3, :]
        ssum = sums[:, 0, :]
        choice = smax[:, 0, 0:ROUNDS * BATCH].rearrange("p (r b) -> p r b", r=ROUNDS)
        work = sb("work", [P, 18, DIM])
        ctx_ring = work[:, 0:8, :]
        stage = work[:, 8:16, :]
        a_ctx = work[:, 0:4, :]
        a_x = work[:, 4:8, :]
        a_xnr = work[:, 8:12, :]
        a_ctxT = work[:, 12:16, :]
        rw_in = work[0:EXPERTS, 15, :]
        a_xnT = work[:, 16:18, :]
        ident = sb("ident", [P, P])
        ident16 = sb("ident16", [P, P], F16)
        before = sb("before", [P, P], F16)
        ones16 = sb("ones16", [P, P], F16)
        iota16 = sb("iota16", [P, P], F16)
        iota_e = sb("iota_e", [P, EXPERTS])
        iota_g = sb("iota_g", [1, GROUPS])
        mark = sb("mark", [P, BATCH], F16)
        quarter = sb("quarter", [P, 4])
        neg_half = sb("neg_half", [P, 2])
        rwT = sb("rwT", [P, HC, EXPERTS])
        b1T = sb("b1T", [P, EXPERTS, FC])
        stats = sb("stats", [P, RING, 2, 6])
        mv = sb("mv", [P, RING, 2, 2])
        veps = sb("veps", [P, RING, 2])
        minus = sb("minus", [P, RING, 2])
        rstd = sb("rstd", [P, RING, 2])
        shift = sb("shift", [P, RING, 2])
        top = sb("top", [P, 2, 2, 8])
        topi = sb("topi", [P, 2, 2, 8], U32)
        warm = sb("warm", [P, 1])
        gap = sb("gap", [P, 2, 2])
        egap = sb("egap", [P, 2, 2])
        den = sb("den", [P, 2, 2])
        psum = stack.enter_context(nc.psum_tensor("psum", [P, 8, 512], F32))

        def slot(b, first, n):
            return slots[:, bass.ds(b * ROW + first, n)]

        def slot2(b, first, n):
            return slots3[:, bass.ds(b, 2), first:first + n]

        def block_of_weights(i0, j):
            return ((psum[:, 4 + 2 * j, :].rearrange("p (q h w) -> p q h w", q=2, h=HC), lambda t: t[:, 2 * j:2 * j + 2, :, bass.ds(i0 * (P // RING), P)]),
                    (psum[:, 5 + 2 * j, :].rearrange("p (f w) -> p f w", f=FC), lambda t: t[:, :, bass.ds(i0 * (DIM // RING) + j * P, P)]))

        def pair_of(dram, b):
            return dram[bass.ds(b, 2), :, :].rearrange("b c l -> c b l")

        s_zero = sem("s_zero")
        s_const = sem("s_const")
        s_rw_in = sem("s_rw_in")
        s_b1_in = sem("s_b1_in")
        s_setT = sem("s_setT")
        s_setc = sem("s_setc")
        m_x_in = sems("m_x_in", RING)
        m_ctx_in = sems("m_ctx_in", RING)
        m_stat = sem("m_stat")
        m_mean = sem("m_mean")
        m_pstep = sem("m_pstep")
        m_norm = sem("m_norm")
        m_q = sem("m_q")
        m_score = sem("m_score")
        m_max = sem("m_max")
        m_top = sem("m_top")
        e_w_in = sems("e_w_in", 2)
        e_wT = sem("e_wT")
        e_whigh = sem("e_whigh")
        e_wlow = sem("e_wlow")
        e_diff = sem("e_diff")
        e_exp = sem("e_exp")
        e_sumv = sem("e_sumv")
        e_sump = sem("e_sump")
        e_total = sem("e_total")
        e_recip = sem("e_recip")
        a_x_in = sems("a_x_in", 2)
        a_ctx_in = sems("a_ctx_in", 2)
        a_ctxTp = sem("a_ctxTp")
        a_ctxTs = sem("a_ctxTs")
        a_probv = sem("a_probv")
        a_probp = sem("a_probp")
        a_pv = sem("a_pv")
        a_x2 = sem("a_x2")
        a_stat = sem("a_stat")
        a_mean = sem("a_mean")
        a_pstep = sem("a_pstep")
        a_norm = sem("a_norm")
        a_xn = sem("a_xn")
        a_high = sem("a_high")
        a_low = sem("a_low")
        a_xnTp = sem("a_xnTp")
        a_xnTs = sem("a_xnTs")
        a_logit = sem("a_logit")
        a_top = sem("a_top")
        a_topi = sem("a_topi")
        a_gap = sem("a_gap")
        a_egap = sem("a_egap")
        a_den = sem("a_den")
        a_p1 = sem("a_p1")
        a_p2 = sem("a_p2")
        a_choice = sem("a_choice")
        a_stored = sems("a_stored", RING)
        r_hot = sem("r_hot")
        r_tot = sem("r_tot")
        r_spread = sem("r_spread")
        r_pos = sem("r_pos")
        r_v = sem("r_v")
        r_ones = sem("r_ones")
        r_tiles = sem("r_tiles")
        r_lane = sem("r_lane")
        r_tileno = sem("r_tileno")
        r_laneno = sem("r_laneno")
        r_list = sem("r_list")
        r_index = sem("r_index")
        r_owner = sem("r_owner")
        r_b2 = sem("r_b2")
        r_b2s = sem("r_b2s")

        taken = [0]

        def take(words, rows=P):
            taken[0] += words
            return slots[0:rows, taken[0] - words:taken[0]]

        N_RBE = ROUNDS * BATCH * EXPERTS
        onehot = take(N_RBE // 2).bitcast(F16)
        totals = take(8)[0:BATCH].bitcast(F16)
        spread = take(N_RBE // 2)[0:BATCH].bitcast(F16)
        place = smax[:, 1:3, :].rearrange("p a b -> p (a b)")
        count_i = take(16).bitcast(I32)
        blocks = take(16)
        ends = take(16)
        ends_half = take(16)
        base = take(16)
        where = take(ROUNDS * BATCH)
        where_i = take(ROUNDS * BATCH).bitcast(I32)
        tile_i = take(ROUNDS * BATCH).bitcast(I32)
        lane_i = take(ROUNDS * BATCH).bitcast(I32)
        tile_of = take(ROUNDS * BATCH // 2).bitcast(F16)
        lane_of = take(ROUNDS * BATCH // 2).bitcast(F16)
        tile_no = take(BATCH * TILES // 2).bitcast(F16)
        lane_no = take(BATCH * P // 2).bitcast(F16)
        lane_hot = take(BATCH * P // 2).bitcast(F16)
        tile_hot = take(BATCH * TILES // 2).bitcast(F16)
        tile_one = take(BATCH * TILES // 2).bitcast(F16)
        passed = take(4 * TILES)
        listed = take(4 * TILES)
        token = take(TILES)
        empty = take(TILES)
        index = take(ROUNDS * GROUPS * 2 * SUB).bitcast(I32)
        past = take(ROUNDS * GROUPS * EXPERTS, 1)
        owner = take(ROUNDS * GROUPS, 1)
        owner_i = take(ROUNDS * GROUPS, 1).bitcast(I32)
        ring_idx = take(LANES * 2 * SUB).bitcast(I32)
        ring_b1 = take(LANES * FC)
        assert taken[0] <= 28 * 2 * ROW
        b2_all = take(EXPERTS * DIM)
        assert taken[0] <= 28 * 2 * ROW
        row_buf = [take(ROW) for _ in range(LANES * SUB)]
        act16 = [[take(FC * GROUP // 2).bitcast(F16) for _ in range(2)] for _ in range(2)]
        assert taken[0] <= BATCH * ROW
        flat = work[:].rearrange("p a b -> p (a b)")
        act32 = [flat[:, j * FC * GROUP:(j + 1) * FC * GROUP] for j in range(2)]
        xT = [flat[:, 2 * FC * GROUP + j * 512:2 * FC * GROUP + (j + 1) * 512].bitcast(F16) for j in range(2)]

        x_rows_in = sems("x_rows_in", LANES)
        x_late_in = sems("x_late_in", L_G2)
        x_out = sems("x_out", LANES)
        x_idx = sem("x_idx")
        x_b1 = sem("x_b1")
        x_tr = sem("x_tr")
        x_xT = sem("x_xT")
        x_hid = sem("x_hid")
        x_act = sem("x_act")
        x_high = sem("x_high")
        x_low = sem("x_low")
        x_y = sem("x_y")
        x_bias = sem("x_bias")
        x_sum = sem("x_sum")
        ALL = ROUNDS * GROUPS
        LIST_BANK = (4, 1)
        LIST_STEP = GROUPS // LANES * LANES

        def is_step(i, k, step):
            return isinstance(i, int) and i + k == step

        def is_late(g):
            return isinstance(g, int) and GROUPS <= g < GROUPS + L_G2

        def late_loads(step):
            first = step - L_G2 + (step > GROUPS + L_G2)
            return [g for g in range(first, step - L_G2 + 2) if is_late(g) and step >= GROUPS + L_G2]

        def hot_lanes(dve, rnd, q):
            b = slice(q * (BATCH // 4), (q + 1) * (BATCH // 4))
            dve.tensor_tensor(lane_hot.rearrange("p (l b) -> p l b", b=BATCH)[:, :, b],
                              lane_of[:, rnd * BATCH:(rnd + 1) * BATCH][:, b].unsqueeze(1).to_broadcast([P, P, BATCH // 4]),
                              lane_no.rearrange("p (l b) -> p l b", b=BATCH)[:, :, b], ALU.is_equal).then_inc(r_lane, 1)

        L_CTX = 2
        L_MAX = 3
        L_SUM, L_LOW = 2, 2
        L_CT, L_PV, L_XN, L_LOWX, L_XNT, L_LG, L_P = 1, 2, 4, 5, 5, 6, 7
        L_XL, L_STORE = 1, 8

        block = stack.enter_context(nc.Block())

        @block.sync
        def _(sp):
            sp.dma_start(rw_in, router_w).then_inc(s_rw_in, 16)
            sp.dma_start(work[0:EXPERTS, 16:18, :].rearrange("e a b -> e (a b)"), b1).then_inc(s_b1_in, 16)

            def load_scores(i, k, n):
                if live(i, k, 0, PAIRS):
                    m, r = i + k, k % RING
                    after(sp, m_mean, m - RING + 1)
                    sp.dma_start(slot2(m * 2, 0, DIM), pair_of(x, m * 2)).then_inc(m_x_in[r], 16)
                if live(i, k, L_CTX, PAIRS):
                    m, r = i + k - L_CTX, (k - L_CTX) % RING
                    after(sp, m_score, m - RING + 1)
                    sp.dma_start(ctx_ring[:, 2 * r:2 * r + 2, :], pair_of(ctx, m * 2)).then_inc(m_ctx_in[r], 16)
            pipeline(sp, PAIRS, RING, 2 * RING, L_CTX, load_scores)

            sp.wait_ge(s_setT, 1)

            def load_exps(i, k, n):
                m, r = i + k, k % RING
                sp.wait_ge(m_score, m + PAIRS - RING + 1)
                sp.dma_start(ctx_ring[:, 2 * r:2 * r + 2, :], pair_of(ctx, m * 2)).then_inc(m_ctx_in[r], 16)
                if k % 2 == 0:
                    j = (k // 2) % 2
                    after(sp, e_wT, n * 2 + k // 2 - 1)
                    sp.dma_start(stage[:, 4 * j:4 * j + 2, :], w1_rows[bass.ds(m * P, 2 * P), :].rearrange("(q p) h -> p q h", p=P)).then_inc(e_w_in[j], 16)
                    sp.dma_start(stage[:, 4 * j + 2:4 * j + 4, :].rearrange("p a b -> p (a b)"), w2_rows[bass.ds(m * (P // 2), P), :]).then_inc(e_w_in[j], 16)
            pipeline(sp, PAIRS, RING, RING, 0, load_exps)

            def attend(i, k, n):
                if live(i, k, 0, PAIRS):
                    m, r = i + k, k % RING
                    if isinstance(i, int) and i + k < RING:
                        sp.wait_ge(m_score, 2 * PAIRS)
                        sp.wait_ge(e_wT, PAIRS // 2)
                    after(sp, a_ctxTp, m - 1)
                    sp.dma_start(a_ctx[:, 2 * (k % 2):2 * (k % 2) + 2, :], pair_of(ctx, m * 2)).then_inc(a_ctx_in[k % 2], 16)
                if live(i, k, L_XL, PAIRS):
                    m, r = i + k - L_XL, (k - L_XL) % 2
                    after(sp, a_x2, m - 1)
                    sp.dma_start(a_x[:, 2 * r:2 * r + 2, :], pair_of(x, m * 2)).then_inc(a_x_in[r], 16)
                if live(i, k, L_STORE, PAIRS):
                    m, r = i + k - L_STORE, (k - L_STORE) % RING
                    before_it = landed_at(i, k - L_STORE, RING) - 16
                    if not isinstance(i, int):
                        sp.lower_val(before_it)
                        sp.lower_val(m + 1)
                    sp.wait_ge(a_low, m + 1)
                    sp.wait_ge(a_p2, m + 1)
                    after(sp, a_stored[r], before_it)
                    sp.dma_start(table_b[bass.ds(m * 2, 2), :, :].rearrange("b c w -> c b w"), slot2(m * 2, 0, ROW)).then_inc(a_stored[r], 16)
            pipeline(sp, PAIRS, RING, 3 * RING, L_STORE, attend)

            for r in range(RING):
                sp.wait_ge(a_stored[r], 16 * 7)
            sp.dma_start(b2_all, b2.rearrange("e (o h) -> o (e h)", o=1).to_broadcast([P, EXPERTS * DIM])).then_inc(r_b2, 16)

        @block.gpsimd
        def _(pool):
            pool.memset(ident[:], 0.0).then_inc(s_zero, 1)
            pool.memset(ident16[:], 0.0).then_inc(s_zero, 1)
            pool.memset(before[:], 0.0).then_inc(s_zero, 1)
            pool.wait_ge(s_zero, 3)
            for mat in (ident, ident16):
                pool.affine_select(out=mat[:], in_=mat[:], pattern=[[-1, P]], compare_op=ALU.not_equal, fill=1.0,
                                   base=0, channel_multiplier=1)
            pool.affine_select(out=before[:], in_=before[:], pattern=[[-1, P]], compare_op=ALU.is_ge, fill=1.0,
                               base=0, channel_multiplier=1)
            pool.memset(neg_half[:], -0.5).then_inc(s_const, 1)

            def norm(ready, m, r, steps, done):
                wait_apart(pool, ready, m + 1)
                pool.tensor_scalar(veps[:, r, :], mv[:, r, :, 1], LN_EPS, None, ALU.add).then_inc(steps, 1)
                pool.tensor_scalar(minus[:, r, :], mv[:, r, :, 0], -1.0, None, ALU.mult).then_inc(steps, 1)
                pool.wait_ge(steps, m * 3 + 2)
                pool.tensor_tensor(rstd[:, r, :], veps[:, r, :], neg_half[:], ALU.pow).then_inc(steps, 1)
                pool.wait_ge(steps, m * 3 + 3)
                pool.tensor_tensor(shift[:, r, :], minus[:, r, :], rstd[:, r, :], ALU.mult).then_inc(done, 1)

            pipeline(pool, PAIRS, RING, RING, 0, lambda i, k, n: norm(m_mean, i + k, k % RING, m_pstep, m_norm))

            pool.memset(ones16[:], 1.0)
            pool.iota(iota16[:], [[1, P]], base=0, channel_multiplier=0, allow_small_or_imprecise_dtypes=True)
            pool.iota(iota_e[:], [[1, EXPERTS]], base=0, channel_multiplier=0, allow_small_or_imprecise_dtypes=True)
            pool.iota(iota_g[:], [[GROUP, GROUPS]], base=0, channel_multiplier=0, allow_small_or_imprecise_dtypes=True)
            pool.iota(mark[:], [[0, 4], [ROWS, BATCH // 4]], base=1, channel_multiplier=1, allow_small_or_imprecise_dtypes=True)
            pool.iota(quarter[:], [[TOKENS // 4, 4]], base=0, channel_multiplier=0, allow_small_or_imprecise_dtypes=True).then_inc(s_const, 1)

            def add_up(i, k, n):
                m = i + k
                pool.wait_ge(e_exp, m + 1)
                if isinstance(m, int) and m == 0:
                    pool.wait_ge(m_top, 1)
                    pool.tensor_copy(sums[:, :, SUM_DVE:], slot2(0, SUM_DVE, 2 * DIM - SUM_DVE)).then_inc(e_sump, 1)
                else:
                    pool.wait_ge(e_sump, m)
                    pool.tensor_tensor(sums[:, :, SUM_DVE:], slot2(m * 2, SUM_DVE, 2 * DIM - SUM_DVE), sums[:, :, SUM_DVE:], ALU.add).then_inc(e_sump, 1)
            pipeline(pool, PAIRS, RING, RING, 0, add_up)

            pool.wait_ge(e_recip, 1)

            def attend(i, k, n):
                if live(i, k, 0, PAIRS):
                    m = i + k
                    pool.tensor_tensor(slot2(m * 2, 0, PROD_POOL), slot2(m * 2, 0, PROD_POOL),
                                       ssum[:, 0:PROD_POOL].unsqueeze(1).to_broadcast([P, 2, PROD_POOL]), ALU.mult).then_inc(a_probp, 1)
                if live(i, k, L_PV, PAIRS):
                    norm(a_mean, i + k - L_PV, (k - L_PV) % RING, a_pstep, a_norm)
            pipeline(pool, PAIRS, RING, 2 * RING, L_PV, attend)

            for r in range(RING):
                pool.wait_ge(a_stored[r], 16 * 7)
            pool.iota(tile_no.rearrange("p (n b) -> p n b", b=BATCH), [[1, TILES], [0, BATCH]], base=0, channel_multiplier=0,
                      allow_small_or_imprecise_dtypes=True).then_inc(r_tileno, 1)

            for r in range(RING):
                pool.wait_ge(a_stored[r], 16 * (PAIRS // RING))
            pool.wait_ge(r_owner, 1)
            pool.wait_ge(r_index, 1)

            def group(i, k, n, rnd):
                if is_step(i, k, GROUPS):
                    pool.wait_ge(r_index, 2)
                if is_step(i, k, GROUPS + L_G2):
                    for r in range(LANES):
                        pool.wait_ge(x_out[r], 32 * len(range(r, GROUPS, LANES)))
                if isinstance(i, int):
                    for g in late_loads(i + k):
                        r = g % LANES
                        pool.wait_ge(x_rows_in[r], 32 * len(range(r, g + 1, LANES)))
                        pool.wait_ge(x_tr, g + 1)
                        for s in range(SUB):
                            pool.indirect_dma_start(row_buf[r * SUB + s], None, table[1],
                                                    bass.IndirectOffsetOnAxis(ap=ring_idx[:, r * 4 + s:r * 4 + s + 1], axis=0)).then_inc(x_late_in[g - GROUPS], 16)
                if live(i, k, 0, ALL):
                    g, r = i + k, k % LANES
                    source = table[1] if round_of(i, k, 0, rnd) == 1 and not is_late(g) else table[0]
                    after(pool, x_out[r], n * 32 + k // LANES * 32)
                    pool.tensor_copy(ring_idx[:, r * 4:r * 4 + 4], index[:, bass.ds(g * 4, 4)]).then_inc(x_idx, 1)
                    pool.wait_ge(x_idx, 1)
                    e = pool.value_load(owner_i[0:1, bass.ds(g, 1)], min_val=0, max_val=EXPERTS - 1)
                    pool.tensor_copy(ring_b1[:, r * FC:(r + 1) * FC], b1T[:].rearrange("p e f -> p (e f)")[:, bass.ds(e * FC, FC)]).then_inc(x_b1, 1)
                    wait_apart(pool, x_idx, g + 1)
                    for s in range(SUB):
                        pool.indirect_dma_start(row_buf[r * SUB + s], None, source,
                                                bass.IndirectOffsetOnAxis(ap=ring_idx[:, r * 4 + s:r * 4 + s + 1], axis=0)).then_inc(x_rows_in[r], 16)
                if live(i, k, L_G2, ALL):
                    g, r = i + k - L_G2, (k - L_G2) % LANES
                    first = round_of(i, k, L_G2, rnd) == 0
                    wait_apart(pool, x_sum, g + 1)
                    for s in range(SUB):
                        rows = row_buf[r * SUB + s] if first else row_buf[r * SUB + s][:, X2:X2 + DIM]
                        pool.indirect_dma_start(table[1] if first else out_rows, bass.IndirectOffsetOnAxis(ap=ring_idx[:, r * 4 + 2 + s:r * 4 + 3 + s], axis=0), rows, None,
                                                bounds_check=TOKENS - 1, oob_is_err=False).then_inc(x_out[r], 16)
            expert_steps(pool, group)
            for r in range(LANES):
                pool.wait_ge(x_out[r], 32 * len(range(r, ALL, LANES)))

        @block.tensor
        def _(pe):
            pe.wait_ge(s_const, 1)
            pe.wait_ge(s_rw_in, 16)
            for h in range(HC):
                mm = pe.transpose(psum[:, 6, h * 8:h * 8 + 8], rw_in[:, h * P:(h + 1) * P], ident[0:8, 0:8])
            pe.wait_ge(s_b1_in, 16)
            for f in range(FC):
                mm = pe.transpose(psum[:, 7, f * 8:f * 8 + 8], work[0:EXPERTS, 16 + f // 2, (f % 2) * P:(f % 2 + 1) * P], ident[0:8, 0:8])
            mm.then_inc(s_setT, 1)

            def score(b, r2, place, done):
                for h in range(HC):
                    mm = pe.matmul(psum[:, r2, h * DIM:(h + 1) * DIM], ctx_ring[:, place, h * P:(h + 1) * P], slot(b, 0, DIM), start=True, stop=True)
                if done:
                    mm.then_inc(m_score, 1)

            def scores_max(i, k, n):
                m, r = i + k, k % RING
                pe.wait_ge(m_ctx_in[r], landed_at(i, k, RING))
                after(pe, m_max, m - 1)
                for j in range(2):
                    pe.wait_ge(m_q, m * 2 + j + 1)
                    score(m * 2 + j, 2 * (k % 2) + j, 2 * r + j, j == 1)
            pipeline(pe, PAIRS, RING, RING, 0, scores_max)

            def scores_exp(i, k, n):
                m, r = i + k, k % RING
                pe.wait_ge(m_ctx_in[r], landed_at(i, k, RING) + 16 * (PAIRS // RING))
                if isinstance(i, int) and i == 0 and k < 2:
                    pe.wait_ge(m_max, PAIRS - 1 + k)
                after(pe, e_diff, m - 1)
                for j in range(2):
                    score(m * 2 + j, 2 * (k % 2) + j, 2 * r + j, j == 1)
                if k % 2 == 0:
                    j = (k // 2) % 2
                    pe.wait_ge(e_w_in[j], n * 32 + 32 * (k // 4) + 32)
                    if isinstance(i, int) and i == 0 and k == 0:
                        pe.wait_ge(s_setc, 1)
                    after(pe, e_wlow, n * 2 + k // 2 - 1)
                    for q in range(2):
                        for h in range(HC):
                            pe.transpose(psum[:, 4 + 2 * j, (q * HC + h) * P:(q * HC + h + 1) * P], stage[:, 4 * j + q, h * P:(h + 1) * P], ident[:])
                    for f in range(FC):
                        mm = pe.transpose(psum[:, 5 + 2 * j, f * P:(f + 1) * P], stage[:, 4 * j + 2 + f // 2, (f % 2) * P:(f % 2 + 1) * P], ident[:])
                    mm.then_inc(e_wT, 1)
            pipeline(pe, PAIRS, RING, RING, 0, scores_exp)

            def attend(i, k, n):
                if isinstance(i, int) and i == 0 and k == 0:
                    pe.wait_ge(e_diff, PAIRS)
                    pe.wait_ge(e_wlow, PAIRS // 2)
                if live(i, k, L_CT, PAIRS):
                    m, r = i + k - L_CT, (k - L_CT) % 2
                    pe.wait_ge(a_ctx_in[r], landed_at(i, k - L_CT, 2))
                    after(pe, a_ctxTs, m - 1)
                    for j in range(2):
                        for h in range(HC):
                            mm = pe.transpose(psum[:, r, (j * HC + h) * P:(j * HC + h + 1) * P], a_ctx[:, 2 * r + j, h * P:(h + 1) * P], ident[:])
                    mm.then_inc(a_ctxTp, 1)
                if live(i, k, L_XNT, PAIRS):
                    m, r = i + k - L_XNT, (k - L_XNT) % 2
                    pe.wait_ge(a_xn, m + 1)
                    after(pe, a_xnTs, m - 1)
                    for j in range(2):
                        for h in range(HC):
                            mm = pe.transpose(psum[:, 4 + r, (j * HC + h) * P:(j * HC + h + 1) * P], a_xnr[:, 2 * r + j, h * P:(h + 1) * P], ident[:])
                    mm.then_inc(a_xnTp, 1)
                if live(i, k, L_LG, PAIRS):
                    m, r = i + k - L_LG, (k - L_LG) % 2
                    pe.wait_ge(a_xnTs, m + 1)
                    after(pe, a_topi, m - 1)
                    for j in range(2):
                        for h in range(HC):
                            mm = pe.matmul(psum[:, 6 + r, j * 8:j * 8 + 8], a_xnT[:, j, h * P:(h + 1) * P], rwT[:, h, :], start=(h == 0), stop=(h == HC - 1))
                    mm.then_inc(a_logit, 1)
                if live(i, k, L_PV, PAIRS):
                    m, r = i + k - L_PV, (k - L_PV) % 2
                    pe.wait_ge(a_ctxTs, m + 1)
                    pe.wait_ge(a_probv, m + 1)
                    pe.wait_ge(a_probp, m + 1)
                    after(pe, a_x2, m - 1)
                    for j in range(2):
                        for h in range(HC):
                            mm = pe.matmul(psum[:, 2 + r, j * DIM:(j + 1) * DIM], a_ctxT[:, 2 * r + j, h * P:(h + 1) * P],
                                           slot(m * 2 + j, h * DIM, DIM), start=(h == 0), stop=(h == HC - 1))
                    mm.then_inc(a_pv, 1)
            pipeline(pe, PAIRS, RING, 2 * RING, L_LG, attend)

            pe.wait_ge(r_hot, 1)
            pe.wait_ge(a_x2, PAIRS)
            pe.wait_ge(s_const, 2)
            hot = onehot.rearrange("p (r b e) -> p r b e", r=ROUNDS, e=EXPERTS)
            for r in range(ROUNDS):
                pe.matmul(psum[:, r, :], before[:], onehot[:, r * 512:(r + 1) * 512], start=True, stop=False)
                for e in range(EXPERTS):
                    mm = pe.matmul(psum[0:BATCH, 2, r * 8 + e:r * 8 + e + 1], hot[:, r, :, e], ones16[:, 0:1], start=True, stop=True)
            mm.then_inc(r_tot, 1)
            pe.wait_ge(r_spread, 1)
            for r in range(ROUNDS):
                pe.matmul(psum[:, r, :], ones16[0:BATCH, :], spread[:, r * 512:(r + 1) * 512], start=False, stop=True)
            pe.matmul(psum[:, 3, 0:16], ones16[0:BATCH, :], totals[:, 0:16], start=True, stop=True).then_inc(r_pos, 1)

            def list_tokens(rnd):
                pe.wait_ge(r_tiles, rnd + 1)
                tiles = tile_hot.rearrange("p (n b) -> p n b", b=BATCH)
                lanes = lane_hot.rearrange("p (l b) -> p l b", b=BATCH)
                w = BATCH // 4
                for b in range(BATCH):
                    q = b // w
                    if b % w == 0:
                        pe.wait_ge(r_lane, 4 * rnd + q + 1)
                    mm = pe.matmul(psum[:, LIST_BANK[rnd], q * TILES:(q + 1) * TILES], lanes[:, :, b], tiles[:, :, b], start=(b % w == 0), stop=(b % w == w - 1))
                mm.then_inc(r_list, 1)

            list_tokens(0)

            def group(i, k, n, rnd):
                if live(i, k, L_G1, ALL):
                    g, r2 = i + k - L_G1, (k - L_G1) % 2
                    e = pe.value_load(owner_i[0:1, bass.ds(g, 1)], min_val=0, max_val=EXPERTS - 1)
                    pe.wait_ge(x_xT, g + 1)
                    after(pe, x_act, g * 2 - 2)
                    for f in range(FC):
                        h = psum[:, 2 + 2 * r2 + f // 2, (f % 2) * GROUP:(f % 2 + 1) * GROUP]
                        for c in range(HC):
                            for px, pw in ((0, 0), (1, 0), (0, 1)):
                                mm = pe.matmul(h, w1T[pw][:, f, c, bass.ds(e * P, P)], xT[r2][:, (px * HC + c) * GROUP:(px * HC + c + 1) * GROUP],
                                               start=(c == 0 and px == 0 and pw == 0), stop=(c == HC - 1 and pw == 1))
                        if f % 2:
                            mm.then_inc(x_hid, 1)
                if live(i, k, L_TR, ALL):
                    g, r = i + k - L_TR, (k - L_TR) % LANES
                    pe.wait_ge(x_rows_in[r], n * 32 + (k - L_TR) // LANES * 32 + 32)
                    after(pe, x_xT, g)
                    bank = psum[:, 0, :].bitcast(F16)
                    for c in range(2 * HC):
                        for s in range(SUB):
                            mm = pe.transpose(bank[:, (c * SUB + s) * P:(c * SUB + s + 1) * P],
                                              row_buf[r * SUB + s][:, XN:XN + DIM].bitcast(F16)[:, c * P:(c + 1) * P], ident16[:])
                    mm.then_inc(x_tr, 1)
                if live(i, k, L_G2, ALL):
                    g, r2 = i + k - L_G2, (k - L_G2) % 2
                    e = pe.value_load(owner_i[0:1, bass.ds(g, 1)], min_val=0, max_val=EXPERTS - 1)
                    pe.wait_ge(x_low, g * 2 + 2)
                    after(pe, x_sum, g - 1)
                    for s in range(SUB):
                        y = psum[:, 6 + r2, s * DIM:(s + 1) * DIM]
                        for f in range(FC):
                            for pa, pw in ((0, 0), (1, 0), (0, 1)):
                                mm = pe.matmul(y, act16[r2][pa][:, f * GROUP + s * P:f * GROUP + (s + 1) * P],
                                               w2T[pw][:, f, bass.ds(e * DIM, DIM)], start=(f == 0 and pa == 0 and pw == 0), stop=(f == FC - 1 and pw == 1))
                    mm.then_inc(x_y, 1)
                if is_step(i, k, LIST_STEP):
                    list_tokens(1)
            pe.wait_ge(r_owner, 1)
            expert_steps(pe, group)

        @block.vector
        def _(dve):
            dve.wait_ge(s_setT, 1)
            dve.tensor_copy(rwT[:].rearrange("p h e -> p (h e)"), psum[:, 6, 0:HC * 8])
            dve.tensor_copy(b1T[:].rearrange("p e f -> p f e"), psum[:, 7, 0:FC * 8].rearrange("p (f e) -> p f e", e=8)).then_inc(s_setc, 1)

            def maximum(i, k, n):
                if live(i, k, 0, PAIRS):
                    m, r = i + k, k % RING
                    wait_apart(dve, m_x_in[r], landed_at(i, k, RING))
                    for j in range(2):
                        dve.bn_stats(stats[:, r, j, :], slot(m * 2 + j, 0, DIM)).then_inc(m_stat, 1)
                if live(i, k, L_MAX, PAIRS):
                    m, r2 = i + k - L_MAX, (k - L_MAX) % 2
                    dve.wait_ge(m_score, m + 1)
                    banks = psum[:, 2 * r2:2 * r2 + 2, :]
                    if isinstance(m, int) and m == 0:
                        dve.tensor_copy(smax[:, 0:2, :], banks).then_inc(m_max, 1)
                    else:
                        dve.wait_ge(m_max, m)
                        dve.tensor_tensor(smax[:, 0:2, :], banks, smax[:, 0:2, :], ALU.max).then_inc(m_max, 1)
                if live(i, k, 0, PAIRS):
                    m, r = i + k, k % RING
                    wait_apart(dve, m_stat, m * 2 + 2)
                    for j in range(2):
                        last = dve.bn_aggr(mv[:, r, j, :], stats[:, r, j, :])
                    last.then_inc(m_mean, 1)
            pipeline(dve, PAIRS, RING, RING, L_MAX, maximum)
            dve.wait_ge(m_max, PAIRS)
            dve.tensor_tensor(smax[:, 0, :], smax[:, 0, :], smax[:, 1, :], ALU.max).then_inc(m_top, 1)
            dve.wait_ge(m_top, 1)

            def exponentials(i, k, n):
                if live(i, k, L_SUM, PAIRS):
                    m = i + k - L_SUM
                    dve.wait_ge(e_exp, m + 1)
                    if isinstance(m, int) and m == 0:
                        dve.tensor_copy(sums[:, :, 0:SUM_DVE], slot2(0, 0, SUM_DVE)).then_inc(e_sumv, 1)
                    else:
                        dve.wait_ge(e_sumv, m)
                        dve.tensor_tensor(sums[:, :, 0:SUM_DVE], slot2(m * 2, 0, SUM_DVE), sums[:, :, 0:SUM_DVE], ALU.add).then_inc(e_sumv, 1)
                if live(i, k, 0, PAIRS):
                    m, r2 = i + k, k % 2
                    dve.wait_ge(m_score, m + PAIRS + 1)
                    dve.tensor_tensor(slot2(m * 2, 0, 2 * DIM), psum[:, 2 * r2:2 * r2 + 2, :],
                                      smax[:, 0:1, :].to_broadcast([P, 2, 2 * DIM]), ALU.subtract).then_inc(e_diff, 1)
                if k % 2 == 0 and live(i, k, L_LOW, PAIRS):
                    j = ((k - L_LOW) // 2) % 2
                    i0 = i + (k - L_LOW) // RING * RING
                    dve.wait_ge(e_whigh, n * 2 + (k - L_LOW) // 2 + 1)
                    (w1_bank, w1_at), (w2_bank, w2_at) = block_of_weights(i0, j)
                    dve.scalar_tensor_tensor(w1_at(w1T[1]), w1_bank, WSCALE, w1_at(w1T[0]), ALU.mult, ALU.subtract)
                    last = dve.scalar_tensor_tensor(w2_at(w2T[1]), w2_bank, WSCALE, w2_at(w2T[0]), ALU.mult, ALU.subtract)
                    last.then_inc(e_wlow, 1)
            pipeline(dve, PAIRS, RING, RING, L_LOW, exponentials)
            dve.wait_ge(e_sumv, PAIRS)
            dve.wait_ge(e_sump, PAIRS)
            dve.tensor_tensor(ssum, ssum, sums[:, 1, :], ALU.add).then_inc(e_total, 1)
            dve.wait_ge(e_total, 1)
            dve.reciprocal(ssum[:, 0:PROD_POOL], ssum[:, 0:PROD_POOL]).then_inc(e_recip, 1)
            dve.reciprocal(ssum[:, PROD_POOL:], ssum[:, PROD_POOL:]).then_inc(e_recip, 1)
            dve.wait_ge(e_recip, 2)

            def attend(i, k, n):
                if live(i, k, L_LOWX, PAIRS):
                    m, r = i + k - L_LOWX, (k - L_LOWX) % 2
                    dve.wait_ge(a_high, m + 1)
                    dve.tensor_tensor(slot2(m * 2, XN + P, P).bitcast(F16), a_xnr[:, 2 * r:2 * r + 2, :], slot2(m * 2, XN, P).bitcast(F16), ALU.subtract).then_inc(a_low, 1)
                if live(i, k, L_P, PAIRS):
                    m, r2 = i + k - L_P, (k - L_P) % 2
                    dve.wait_ge(a_egap, m + 1)
                    dve.tensor_scalar(den[:, r2, :], egap[:, r2, :], WSCALE, WSCALE, ALU.mult, ALU.add).then_inc(a_den, 1)
                if live(i, k, L_LG, PAIRS):
                    m, r2 = i + k - L_LG, (k - L_LG) % 2
                    wait_apart(dve, a_logit, m + 1)
                    for j in range(2):
                        last = dve.max(top[:, r2, j, :], psum[:, 6 + r2, j * 8:j * 8 + 8])
                    last.then_inc(a_top, 1)
                if live(i, k, L_PV, PAIRS):
                    m, r = i + k - L_PV, (k - L_PV) % 2
                    dve.wait_ge(a_pv, m + 1)
                    dve.wait_ge(a_x_in[r], landed_at(i, k - L_PV, 2))
                    dve.tensor_tensor(slot2(m * 2, X2, DIM), psum[:, 2 + r, :].rearrange("p (b w) -> p b w", b=2), a_x[:, 2 * r:2 * r + 2, :], ALU.add).then_inc(a_x2, 1)
                if live(i, k, L_P, PAIRS):
                    m, r2 = i + k - L_P, (k - L_P) % 2
                    dve.wait_ge(a_den, m + 1)
                    dve.reciprocal(slot2(m * 2, PR, 1).rearrange("p b w -> p (b w)"), den[:, r2, :]).then_inc(a_p1, 1)
                if live(i, k, L_LG, PAIRS):
                    m, r2 = i + k - L_LG, (k - L_LG) % 2
                    wait_apart(dve, a_top, m + 1)
                    dve.tensor_tensor(gap[:, r2, :], top[:, r2, :, 1], top[:, r2, :, 0], ALU.subtract).then_inc(a_gap, 1)
                    for j in range(2):
                        last = dve.max_index(topi[:, r2, j, :], top[:, r2, j, :], psum[:, 6 + r2, j * 8:j * 8 + 8])
                    last.then_inc(a_topi, 1)
                if live(i, k, L_PV, PAIRS):
                    m, r4 = i + k - L_PV, (k - L_PV) % RING
                    wait_apart(dve, a_x2, m + 1)
                    for j in range(2):
                        last = dve.bn_stats(stats[:, r4, j, :], slot(m * 2 + j, X2, DIM))
                    last.then_inc(a_stat, 1)
                if live(i, k, L_P, PAIRS):
                    m, r2 = i + k - L_P, (k - L_P) % 2
                    dve.wait_ge(a_p1, m + 1)
                    dve.tensor_tensor(slot2(m * 2, PR + 1, 1).rearrange("p b w -> p (b w)"), slot2(m * 2, PR, 1).rearrange("p b w -> p (b w)"),
                                      egap[:, r2, :], ALU.mult).then_inc(a_p2, 1)
                if live(i, k, L_LG, PAIRS):
                    m, r2 = i + k - L_LG, (k - L_LG) % 2
                    dve.wait_ge(a_topi, m + 1)
                    dve.tensor_copy(choice[:, :, bass.ds(m * 2, 2)], topi[:, r2, :, 0:ROUNDS].rearrange("p b r -> p r b")).then_inc(a_choice, 1)
                if live(i, k, L_PV, PAIRS):
                    m, r4 = i + k - L_PV, (k - L_PV) % RING
                    wait_apart(dve, a_stat, m + 1)
                    for j in range(2):
                        last = dve.bn_aggr(mv[:, r4, j, :], stats[:, r4, j, :])
                    last.then_inc(a_mean, 1)
                if live(i, k, 0, PAIRS):
                    m = i + k
                    dve.tensor_tensor(slot2(m * 2, PROD_POOL, 2 * DIM - PROD_POOL), slot2(m * 2, PROD_POOL, 2 * DIM - PROD_POOL),
                                      ssum[:, PROD_POOL:].unsqueeze(1).to_broadcast([P, 2, 2 * DIM - PROD_POOL]), ALU.mult).then_inc(a_probv, 1)
            pipeline(dve, PAIRS, RING, 2 * RING, L_P, attend)

            steps = [0]

            def chain(*ops):
                steps[0] += len(ops)
                for op in ops:
                    op.then_inc(r_v, 1)
                dve.wait_ge(r_v, steps[0])

            for r in range(RING):
                dve.wait_ge(a_stored[r], 16 * 7)
            dve.wait_ge(s_const, 2)
            dve.wait_ge(a_choice, PAIRS)
            hot = onehot.rearrange("p (r b e) -> p r b e", r=ROUNDS, e=EXPERTS)
            dve.tensor_tensor(hot, choice.unsqueeze(3).to_broadcast([P, ROUNDS, BATCH, EXPERTS]),
                              iota_e[:].unsqueeze(1).unsqueeze(1).to_broadcast([P, ROUNDS, BATCH, EXPERTS]), ALU.is_equal).then_inc(r_hot, 1)
            dve.wait_ge(r_tot, 1)
            chain(dve.tensor_copy(totals[:, 0:16], psum[0:BATCH, 2, 0:16]))
            dve.tensor_tensor(spread.rearrange("p (r b e) -> p r b e", r=ROUNDS, e=EXPERTS),
                              totals[:, 0:16].rearrange("p (r e) -> p r e", r=ROUNDS).unsqueeze(2).to_broadcast([BATCH, ROUNDS, BATCH, EXPERTS]),
                              before[0:BATCH, 0:BATCH].unsqueeze(1).unsqueeze(3).to_broadcast([BATCH, ROUNDS, BATCH, EXPERTS]),
                              ALU.mult).then_inc(r_spread, 1)
            dve.wait_ge(r_pos, 1)
            chain(dve.tensor_scalar(count_i, psum[:, 3, 0:16], float(GROUP - 1), None, ALU.add))
            chain(dve.tensor_scalar(count_i, count_i, GROUP.bit_length() - 1, None, ALU.arith_shift_right))
            chain(dve.tensor_scalar(blocks, count_i, float(GROUP), None, ALU.mult))
            blk = blocks.rearrange("p (r e) -> p r e", r=ROUNDS)
            end = ends.rearrange("p (r e) -> p r e", r=ROUNDS)
            half_end = ends_half.rearrange("p (r e) -> p r e", r=ROUNDS)
            source, other = blk, [end, half_end]
            for far in (1, 2, 4):
                upto = other[far == 2]
                chain(dve.tensor_copy(upto[:, :, 0:far], source[:, :, 0:far]),
                      dve.tensor_tensor(upto[:, :, far:], source[:, :, far:], source[:, :, 0:EXPERTS - far], ALU.add))
                source = upto
            chain(dve.tensor_tensor(base, ends, blocks, ALU.subtract))
            pl = place.rearrange("p (r b e) -> p r b e", r=ROUNDS, e=EXPERTS)

            def place_tokens(r):
                ph, cols = slice(r * BATCH * EXPERTS, (r + 1) * BATCH * EXPERTS), slice(r * BATCH, (r + 1) * BATCH)
                chain(dve.tensor_tensor(pl[:, r], psum[:, r, :].rearrange("p (b e) -> p b e", e=EXPERTS),
                                        base[:, r * 8:r * 8 + 8].unsqueeze(1).to_broadcast([P, BATCH, EXPERTS]), ALU.add))
                chain(dve.tensor_tensor(place[:, ph], place[:, ph], onehot[:, ph], ALU.mult))
                chain(dve.tensor_reduce(where[:, cols], pl[:, r], AX_X, ALU.add))
                chain(dve.tensor_copy(where_i[:, cols], where[:, cols]))
                chain(dve.tensor_scalar(tile_i[:, cols], where_i[:, cols], 7, None, ALU.arith_shift_right),
                      dve.tensor_scalar(lane_i[:, cols], where_i[:, cols], P - 1, None, ALU.bitwise_and))
                chain(dve.tensor_copy(tile_of[:, cols], tile_i[:, cols]), dve.tensor_copy(lane_of[:, cols], lane_i[:, cols]))

            def hot_tiles(rnd):
                dve.tensor_tensor(tile_one.rearrange("p (n b) -> p n b", b=BATCH),
                                  tile_of[:, rnd * BATCH:(rnd + 1) * BATCH].unsqueeze(1).to_broadcast([P, TILES, BATCH]),
                                  tile_no.rearrange("p (n b) -> p n b", b=BATCH), ALU.is_equal).then_inc(r_ones, 1)

            def mark_tiles(rnd):
                dve.wait_ge(r_ones, rnd + 1)
                dve.tensor_tensor(tile_hot.rearrange("p (n b) -> p n b", b=BATCH), tile_one.rearrange("p (n b) -> p n b", b=BATCH),
                                  mark[:].unsqueeze(1).to_broadcast([P, TILES, BATCH]), ALU.mult).then_inc(r_tiles, 1)

            def indices(rnd):
                dve.wait_ge(r_list, rnd + 1)
                bank = psum[:, LIST_BANK[rnd], 0:4 * TILES]
                by_quarter = "p (q n) -> p q n"
                chain(dve.scalar_tensor_tensor(passed.rearrange(by_quarter, q=4), bank.rearrange(by_quarter, q=4), 0.0,
                                               quarter[:].unsqueeze(2).to_broadcast([P, 4, TILES]), ALU.is_gt, ALU.mult))
                chain(dve.tensor_tensor(listed, bank, passed, ALU.add))
                chain(dve.tensor_reduce(token, listed.rearrange("p (q n) -> p n q", q=4), AX_X, ALU.add))
                ix = index.rearrange("p (r n w s) -> p r n w s", r=ROUNDS, w=2, s=SUB)[:, rnd]
                chain(dve.tensor_scalar(empty, token, 0.0, float(SKIPPED), ALU.is_equal, ALU.mult),
                      dve.tensor_scalar(ix[:, :, 0, :], token.rearrange("p (n s) -> p n s", s=SUB), -1.0, 0.0, ALU.add, ALU.max))
                dve.scalar_tensor_tensor(ix[:, :, 1, :], token.rearrange("p (n s) -> p n s", s=SUB), -1.0, empty.rearrange("p (n s) -> p n s", s=SUB),
                                         ALU.add, ALU.add).then_inc(r_index, 1)

            place_tokens(0)
            dve.wait_ge(r_tileno, 1)
            dve.wait_ge(r_laneno, 1)
            hot_tiles(0)
            mark_tiles(0)
            for q in range(4):
                hot_lanes(dve, 0, q)
            pst = past.rearrange("p (r g e) -> p r g e", r=ROUNDS, e=EXPERTS)
            chain(*[dve.tensor_tensor(pst[:, r], ends[0:1, r * 8:r * 8 + 8].unsqueeze(1).to_broadcast([1, GROUPS, EXPERTS]),
                                      iota_g[:].unsqueeze(2).to_broadcast([1, GROUPS, EXPERTS]), ALU.is_le) for r in range(ROUNDS)])
            chain(dve.tensor_reduce(owner, past.rearrange("p (n e) -> p n e", e=EXPERTS), AX_X, ALU.add))
            dve.tensor_scalar(owner_i, owner, float(EXPERTS - 1), None, ALU.min).then_inc(r_owner, 1)
            indices(0)
            place_tokens(1)

            dve.wait_ge(r_b2s, 1)

            def add_bias(g, r, count, now):
                e = dve.value_load(owner_i[0:1, bass.ds(g, 1)], min_val=0, max_val=EXPERTS - 1)
                dve.wait_ge(x_rows_in[r], count)
                for s in range(SUB):
                    rows = row_buf[r * SUB + s]
                    last = dve.scalar_tensor_tensor(rows[:, X2:X2 + DIM], b2_all[:, bass.ds(e * DIM, DIM)], rows[:, PR + now:PR + now + 1],
                                                    rows[:, X2:X2 + DIM], ALU.mult, ALU.add)
                last.then_inc(x_bias, 1)

            def group(i, k, n, rnd):
                if live(i, k, L_G1, ALL):
                    g, r, r2 = i + k - L_G1, (k - L_G1) % LANES, (k - L_G1) % 2
                    after(dve, x_y, g - 1)
                    for j in range(2):
                        dve.wait_ge(x_act, g * 2 + j + 1)
                        cols = slice(j * 2 * GROUP, (j + 1) * 2 * GROUP)
                        dve.tensor_copy(act16[r2][0][:, cols], act32[r2][:, cols]).then_inc(x_high, 1)
                        dve.wait_ge(x_high, g * 2 + j + 1)
                        dve.tensor_tensor(act16[r2][1][:, cols], act32[r2][:, cols], act16[r2][0][:, cols], ALU.subtract).then_inc(x_low, 1)
                    if not is_late(g):
                        add_bias(g, r, n * 32 + (k - L_G1) // LANES * 32 + 32, round_of(i, k, L_G1, rnd))
                if live(i, k, L_G2, ALL):
                    g, r, r2 = i + k - L_G2, (k - L_G2) % LANES, (k - L_G2) % 2
                    now = round_of(i, k, L_G2, rnd)
                    if is_late(g):
                        dve.wait_ge(x_late_in[g - GROUPS], 32)
                        add_bias(g, r, 32 * len(range(r, g + 1, LANES)), now)
                    dve.wait_ge(x_bias, g + 1 + (is_late(g) and not is_late(g + 1)))
                    dve.wait_ge(x_y, g + 1)
                    for s in range(SUB):
                        rows = row_buf[r * SUB + s]
                        last = dve.scalar_tensor_tensor(rows[:, X2:X2 + DIM], psum[:, 6 + r2, s * DIM:(s + 1) * DIM], rows[:, PR + now:PR + now + 1],
                                                        rows[:, X2:X2 + DIM], ALU.mult, ALU.add)
                    last.then_inc(x_sum, 1)
                if is_step(i, k, 0):
                    dve.wait_ge(r_tiles, 1)
                    hot_tiles(1)
                if is_step(i, k, 1):
                    dve.wait_ge(r_list, 1)
                    mark_tiles(1)
                if isinstance(i, int) and 2 <= i + k < 6:
                    hot_lanes(dve, 1, i + k - 2)
                if is_step(i, k, LIST_STEP + 1):
                    indices(1)
            expert_steps(dve, group)

        @block.scalar
        def _(act):
            def queries(i, k, n):
                m, r = i + k, k % RING
                act.wait_ge(m_norm, m + 1)
                for j in range(2):
                    act.activation(slot(m * 2 + j, 0, DIM), slot(m * 2 + j, 0, DIM), ACT.Identity, bias=shift[:, r, j:j + 1],
                                   scale=rstd[:, r, j:j + 1]).then_inc(m_q, 1)
            pipeline(act, PAIRS, RING, RING, 0, queries)

            def exponentials(i, k, n):
                m = i + k
                act.wait_ge(e_diff, m + 1)
                act.activation(slot2(m * 2, 0, 2 * DIM), slot2(m * 2, 0, 2 * DIM), ACT.Exp, scale=SCORE_SCALE).then_inc(e_exp, 1)
                if k % 2 == 0:
                    j = (k // 2) % 2
                    i0 = i + k // RING * RING
                    act.wait_ge(e_wT, n * 2 + k // 2 + 1)
                    (w1_bank, w1_at), (w2_bank, w2_at) = block_of_weights(i0, j)
                    act.activation(w1_at(w1T[0]), w1_bank, ACT.Copy, scale=WSCALE)
                    last = act.activation(w2_at(w2T[0]), w2_bank, ACT.Copy, scale=WSCALE)
                    last.then_inc(e_whigh, 1)
            pipeline(act, PAIRS, RING, RING, 0, exponentials)

            def attend(i, k, n):
                if live(i, k, L_CT, PAIRS):
                    m, r = i + k - L_CT, (k - L_CT) % 2
                    act.wait_ge(a_ctxTp, m + 1)
                    after(act, a_pv, m - 1)
                    if isinstance(m, int) and m == 0:
                        act.wait_ge(e_wT, PAIRS // 2)
                    act.activation(a_ctxT[:, 2 * r:2 * r + 2, :].rearrange("p a b -> p (a b)"), psum[:, r, :], ACT.Copy).then_inc(a_ctxTs, 1)
                if live(i, k, L_XN, PAIRS):
                    m, r, r4 = i + k - L_XN, (k - L_XN) % 2, (k - L_XN) % RING
                    after(act, a_low, m - 1)
                    after(act, a_xnTp, m - 1)
                    act.wait_ge(a_norm, m + 1)
                    for j in range(2):
                        last = act.activation(a_xnr[:, 2 * r + j, :], slot(m * 2 + j, X2, DIM), ACT.Identity, bias=shift[:, r4, j:j + 1], scale=rstd[:, r4, j:j + 1])
                    last.then_inc(a_xn, 1)
                if live(i, k, L_XNT, PAIRS):
                    m, r = i + k - L_XNT, (k - L_XNT) % 2
                    act.wait_ge(a_xnTp, m + 1)
                    after(act, a_logit, m)
                    act.activation(a_xnT.rearrange("p a b -> p (a b)"), psum[:, 4 + r, :], ACT.Copy).then_inc(a_xnTs, 1)
                if live(i, k, L_XN, PAIRS):
                    m, r = i + k - L_XN, (k - L_XN) % 2
                    act.wait_ge(a_xn, m + 1)
                    act.activation(slot2(m * 2, XN, P).bitcast(F16), a_xnr[:, 2 * r:2 * r + 2, :], ACT.Copy).then_inc(a_high, 1)
                if live(i, k, L_LG, PAIRS):
                    m, r2 = i + k - L_LG, (k - L_LG) % 2
                    act.wait_ge(a_gap, m + 1)
                    act.activation(egap[:, r2, :], gap[:, r2, :], ACT.Exp).then_inc(a_egap, 1)
            pipeline(act, PAIRS, RING, 2 * RING, L_LG, attend)

            for r in range(RING):
                act.wait_ge(a_stored[r], 16 * 7)
            act.wait_ge(s_const, 2)
            act.activation(lane_no.rearrange("p (l b) -> p l b", b=BATCH), iota16[:].unsqueeze(2).to_broadcast([P, P, BATCH]), ACT.Copy).then_inc(r_laneno, 1)
            act.wait_ge(r_b2, 16)
            act.activation(b2_all, b2_all, ACT.Copy, scale=WSCALE).then_inc(r_b2s, 1)

            act.activation(warm[:], neg_half[:, 0:1], ACT.Gelu)

            def group(i, k, n, rnd):
                if live(i, k, L_G1, ALL):
                    g, r, r2 = i + k - L_G1, (k - L_G1) % LANES, (k - L_G1) % 2
                    act.wait_ge(x_b1, g + 1)
                    after(act, x_low, g * 2 - 2)
                    for f in range(FC):
                        if f % 2 == 0:
                            act.wait_ge(x_hid, g * 2 + f // 2 + 1)
                        last = act.activation(act32[r2][:, f * GROUP:(f + 1) * GROUP], psum[:, 2 + 2 * r2 + f // 2, (f % 2) * GROUP:(f % 2 + 1) * GROUP],
                                              ACT.Gelu, bias=ring_b1[:, r * FC + f:r * FC + f + 1], scale=1.0 / WSCALE)
                        if f % 2:
                            last.then_inc(x_act, 1)
                if live(i, k, L_TR, ALL):
                    g, r2 = i + k - L_TR, (k - L_TR) % 2
                    act.wait_ge(x_tr, g + 1)
                    after(act, x_hid, g * 2 - 2)
                    act.activation(xT[r2], psum[:, 0, :].bitcast(F16), ACT.Copy).then_inc(x_xT, 1)
            expert_steps(act, group)


_INS = ["x", "ctx_1024", "L0_ffn_router_w", "L0_ffn_w1", "L0_ffn_b1", "L0_ffn_w2", "L0_ffn_b2"]


def kernel(**inputs):
    import numpy as np
    import concourse.bacc as bacc
    from concourse.bass_utils import run_bass_kernel_spmd

    nc = bacc.Bacc("TRN2", target_bir_lowering=False, num_devices=1, dynamic_dma_scratch_size=4096)
    arrays, args = {}, []
    for name in _INS:
        a = np.ascontiguousarray(inputs[name])
        arrays[f"in_{name}"] = a
        args.append(nc.dram_tensor(f"in_{name}", a.shape, mybir.dt.from_np(a.dtype), kind="ExternalInput").ap())
    args.append(nc.dram_tensor("out_x", (BATCH, ROWS, DIM), F32, kind="ExternalOutput").ap())
    xattn_ffn(nc, *args)
    return run_bass_kernel_spmd(nc, [arrays], core_ids=[0]).results[0]["out_x"]
```
